# Optimizing a Trainium2 kernel written in Bass

```python
import numpy as np
import jax
import jax.numpy as jnp

def _softmax(x, axis=-1):
    return jax.nn.softmax(x, axis=axis)

def _gelu(x):
    return jax.nn.gelu(x, approximate=True)

def _silu(x):
    return jax.nn.silu(x)

def _sigmoid(x):
    return jax.nn.sigmoid(x)

def _layernorm(x, axis=-1, eps=1e-05):
    m = jnp.mean(x, axis=axis, keepdims=True)
    v = jnp.var(x, axis=axis, keepdims=True)
    return (x - m) / jnp.sqrt(v + eps)

def _scatter_add(tgt, idx, src, axis=0):
    return tgt.at[idx].add(src)

def _segment_sum(src, seg, n):
    return jax.ops.segment_sum(src, seg, n)
kernel_name = 'mk_prb_d1_jaxref_r8_79b53e'

def setup_inputs(seed: int=0):
    np.random.seed(seed)
    _w = jnp.asarray

    def _L0_attn_setup():
        import jax, jax.numpy as jnp
        import numpy as np
        import math
        B, N, DIM, H, DH, NNULL = (2, 256, 128, 16, 64, 2)
        SCALE = 8.0
        LN_EPS = 1e-05

        def _alibi_slopes(heads):
            start = 2.0 ** (-2.0 ** (-(math.log2(heads) - 3)))
            return np.array([start * start ** i for i in range(heads)], dtype=np.float32)

        def _l2norm(t):
            n = jnp.sqrt(jnp.sum(t * t, axis=-1, keepdims=True))
            return t / jnp.maximum(n, 1e-12)
        key = jax.random.key(seed)
        ks = jax.random.split(key, 6)
        inner = H * DH
        return {'x': jax.random.normal(ks[0], (B, N, DIM), dtype=jnp.float32), 'norm_g': jnp.ones((DIM,), jnp.float32), 'norm_b': jnp.zeros((DIM,), jnp.float32), 'Wq': jax.random.normal(ks[1], (DIM, inner), jnp.float32) * 0.02, 'Wkv': jax.random.normal(ks[2], (DIM, 2 * inner), jnp.float32) * 0.02, 'q_scale': jnp.ones((DH,), jnp.float32), 'k_scale': jnp.ones((DH,), jnp.float32), 'null_kv': jax.random.normal(ks[3], (H, 2 * NNULL, DH), jnp.float32), 'Wout': jax.random.normal(ks[4], (inner, DIM), jnp.float32) * 0.02}
    _L0_attn_in = _L0_attn_setup()

    def _L0_ffn_setup():
        import jax, jax.numpy as jnp
        import numpy as np
        H = 128
        I = 256
        E = 8
        TOP_K = 2
        NUM_SHARED = 1
        key = jax.random.key(seed)
        ks = jax.random.split(key, 9)
        s = 0.02
        x = jax.random.normal(ks[0], (2, 256, H), dtype=jnp.float32)
        sg_w = jax.random.normal(ks[1], (I, H), dtype=jnp.float32) * s
        su_w = jax.random.normal(ks[2], (I, H), dtype=jnp.float32) * s
        sd_w = jax.random.normal(ks[3], (H, I), dtype=jnp.float32) * s
        router_w = jax.random.normal(ks[4], (E, H), dtype=jnp.float32) * s
        routing_bias = jnp.zeros((E,), dtype=jnp.float32)
        wg = jax.random.normal(ks[5], (E, I, H), dtype=jnp.float32) * s
        wu = jax.random.normal(ks[6], (E, I, H), dtype=jnp.float32) * s
        wd = jax.random.normal(ks[7], (E, H, I), dtype=jnp.float32) * s
        return {'x': x, 'sg_w': sg_w, 'su_w': su_w, 'sd_w': sd_w, 'router_w': router_w, 'routing_bias': routing_bias, 'wg': wg, 'wu': wu, 'wd': wd}
    _L0_ffn_in = _L0_ffn_setup()
    _d = {'L0_attn_x': _L0_attn_in['x'], 'L0_attn_norm_g': _L0_attn_in['norm_g'], 'L0_attn_norm_b': _L0_attn_in['norm_b'], 'L0_attn_Wq': _L0_attn_in['Wq'], 'L0_attn_Wkv': _L0_attn_in['Wkv'], 'L0_attn_q_scale': _L0_attn_in['q_scale'], 'L0_attn_k_scale': _L0_attn_in['k_scale'], 'L0_attn_null_kv': _L0_attn_in['null_kv'], 'L0_attn_Wout': _L0_attn_in['Wout'], 'L0_ffn_sg_w': _L0_ffn_in['sg_w'], 'L0_ffn_su_w': _L0_ffn_in['su_w'], 'L0_ffn_sd_w': _L0_ffn_in['sd_w'], 'L0_ffn_router_w': _L0_ffn_in['router_w'], 'L0_ffn_routing_bias': _L0_ffn_in['routing_bias'], 'L0_ffn_wg': _L0_ffn_in['wg'], 'L0_ffn_wu': _L0_ffn_in['wu'], 'L0_ffn_wd': _L0_ffn_in['wd']}
    _x0 = _d['L0_attn_x']
    _d['L0_attn_x'] = jax.random.normal(jax.random.fold_in(jax.random.key(seed), 1), (8, 256, 128), dtype=_x0.dtype)
    del _x0
    return _d

def reference(L0_attn_x, L0_attn_norm_g, L0_attn_norm_b, L0_attn_Wq, L0_attn_Wkv, L0_attn_q_scale, L0_attn_k_scale, L0_attn_null_kv, L0_attn_Wout, L0_ffn_sg_w, L0_ffn_su_w, L0_ffn_sd_w, L0_ffn_router_w, L0_ffn_routing_bias, L0_ffn_wg, L0_ffn_wu, L0_ffn_wd):

    def _L0_attn_ref(x, norm_g, norm_b, Wq, Wkv, q_scale, k_scale, null_kv, Wout):
        import jax, jax.numpy as jnp
        import numpy as np
        import math
        B, N, DIM, H, DH, NNULL = (2, 256, 128, 16, 64, 2)
        SCALE = 8.0
        LN_EPS = 1e-05

        def _alibi_slopes(heads):
            start = 2.0 ** (-2.0 ** (-(math.log2(heads) - 3)))
            return np.array([start * start ** i for i in range(heads)], dtype=np.float32)

        def _l2norm(t):
            n = jnp.sqrt(jnp.sum(t * t, axis=-1, keepdims=True))
            return t / jnp.maximum(n, 1e-12)
        b, n, dim = x.shape
        h, dh, nn = (H, DH, NNULL)
        j = n + nn
        mu = jnp.mean(x, axis=-1, keepdims=True)
        var = jnp.mean((x - mu) ** 2, axis=-1, keepdims=True)
        xn = (x - mu) * jax.lax.rsqrt(var + LN_EPS) * norm_g + norm_b
        q = (xn @ Wq).reshape(b, n, h, dh).transpose(0, 2, 1, 3)
        kv = x @ Wkv
        k, v = jnp.split(kv, 2, axis=-1)
        k = k.reshape(b, n, h, dh).transpose(0, 2, 1, 3)
        v = v.reshape(b, n, h, dh).transpose(0, 2, 1, 3)
        null = null_kv.reshape(h, nn, 2, dh)
        nk = jnp.broadcast_to(null[:, :, 0, :][None], (b, h, nn, dh))
        nv = jnp.broadcast_to(null[:, :, 1, :][None], (b, h, nn, dh))
        k = jnp.concatenate([nk, k], axis=2)
        v = jnp.concatenate([nv, v], axis=2)
        q = _l2norm(q) * q_scale
        k = _l2norm(k) * k_scale
        sim = jnp.einsum('bhid,bhjd->bhij', q, k) * SCALE
        irow = jnp.arange(j - n, j)
        jcol = jnp.arange(j)
        bias = -jnp.abs(jcol[None, :] - irow[:, None]).astype(sim.dtype)
        slopes = jnp.asarray(_alibi_slopes(h))[:, None, None]
        sim = sim + slopes * bias
        causal = jnp.triu(jnp.ones((n, j), dtype=bool), k=j - n + 1)
        neg = jnp.finfo(sim.dtype).max
        sim = jnp.where(causal[None, None], -neg, sim)
        attn = jax.nn.softmax(sim, axis=-1)
        out = jnp.einsum('bhij,bhjd->bhid', attn, v)
        out = out.transpose(0, 2, 1, 3).reshape(b, n, h * dh)
        return out @ Wout

    def _L0_ffn_ref(x, sg_w, su_w, sd_w, router_w, routing_bias, wg, wu, wd):
        import jax, jax.numpy as jnp
        import numpy as np
        H = 128
        I = 256
        E = 8
        TOP_K = 2
        NUM_SHARED = 1
        orig_shape = x.shape
        xt = x.reshape(-1, H)
        T = xt.shape[0]
        shared = jax.nn.silu(xt @ sg_w.T) * (xt @ su_w.T) @ sd_w.T
        shared = shared / NUM_SHARED
        logits = xt @ router_w.T + routing_bias
        probs = jax.nn.sigmoid(logits)
        topk_p, topk_idx = jax.lax.top_k(probs, TOP_K)
        topk_p = topk_p / jnp.sum(topk_p, axis=-1, keepdims=True)
        w = jnp.zeros((T, E), dtype=xt.dtype)
        w = w.at[jnp.arange(T)[:, None], topk_idx].add(topk_p)
        g = jnp.einsum('th,eih->tei', xt, wg)
        u = jnp.einsum('th,eih->tei', xt, wu)
        h = jax.nn.silu(g) * u
        y = jnp.einsum('tei,ehi->teh', h, wd)
        routed = jnp.einsum('te,teh->th', w, y)
        return (shared + routed).reshape(orig_shape)
    x = L0_attn_x
    xn = _layernorm(x, axis=-1)
    x = x + _L0_attn_ref(xn, L0_attn_norm_g, L0_attn_norm_b, L0_attn_Wq, L0_attn_Wkv, L0_attn_q_scale, L0_attn_k_scale, L0_attn_null_kv, L0_attn_Wout) + _L0_ffn_ref(xn, L0_ffn_sg_w, L0_ffn_su_w, L0_ffn_sd_w, L0_ffn_router_w, L0_ffn_routing_bias, L0_ffn_wg, L0_ffn_wu, L0_ffn_wd)
    return x

_drawn_inputs = setup_inputs


def setup_inputs(seed=0):
    import zlib

    import numpy as np

    out = dict(_drawn_inputs(seed))
    spreads = {'L0_attn_norm_g': (1.0, 0.6),
     'L0_attn_norm_b': (0.0, 2.0),
     'L0_attn_q_scale': (1.0, 0.6),
     'L0_attn_k_scale': (1.0, 0.6),
     'L0_ffn_routing_bias': (0.0, 0.8)}
    factors = {'L0_ffn_sg_w': 6.493,
     'L0_ffn_su_w': 6.179,
     'L0_ffn_sd_w': 6.112,
     'L0_ffn_router_w': 8.0,
     'L0_ffn_wg': 8.0,
     'L0_ffn_wu': 8.0,
     'L0_ffn_wd': 8.0,
     'L0_attn_Wq': 3.545,
     'L0_attn_Wkv': 3.541,
     'L0_attn_null_kv': 5.295,
     'L0_attn_Wout': 3.157}
    for name, (base, spread) in spreads.items():
        noise = np.random.default_rng([zlib.crc32(name.encode()), seed]).standard_normal(out[name].shape)
        drawn = base * np.exp(spread * noise) if base else spread * noise
        out[name] = jnp.asarray(drawn.astype(out[name].dtype))
    for name, factor in factors.items():
        out[name] = (out[name] * factor).astype(out[name].dtype)
    return out
```

```python
from contextlib import ExitStack

import concourse.bass as bass
from concourse import mybir

F32 = mybir.dt.float32
F32R = mybir.dt.float32r
BF16 = mybir.dt.bfloat16
I32 = mybir.dt.int32
U32 = mybir.dt.uint32
ALU = mybir.AluOpType
ACT = mybir.ActivationFunctionType
AX = mybir.AxisListType

P = 128
BATCH, SEQ, DIM = 8, 256, 128
HEADS, DH, NNULL = 16, 64, 2
INNER = HEADS * DH
E, I, TOPK = 8, 256, 2
NT = BATCH * SEQ // P
TB = SEQ // P
PAIRS = HEADS // 2
K0 = NNULL + P
K1 = NNULL + SEQ
KS = K0 + K1
SIM_SCALE = 8.0
LN_EPS = 1e-5
L2_EPS2 = 1e-24
MASKED = -1e30
SLOPES = [2.0 ** (-0.5 * (h + 1)) for h in range(HEADS)]
MU = 8
SLOT_TILES = -(-(NT * TOPK + E - 1) // MU) * MU
SLOTS = SLOT_TILES * P


def build(nc, a, out):
    with ExitStack() as ctx:
        def sb(name, shape, dt=F32):
            return ctx.enter_context(nc.sbuf_tensor(name, shape, dt))

        def sem(name):
            return ctx.enter_context(nc.semaphore(name))

        bank = [ctx.enter_context(nc.psum_tensor(f"bank{i}", [P, 512], F32)) for i in range(8)]

        xg_dram = nc.dram_tensor("slot_x", [SLOTS, DIM], F32).ap()
        yg_dram = nc.dram_tensor("slot_y", [SLOTS, DIM], F32).ap()

        xn1T = sb("xn1T", [P, NT * P])
        xn2T = sb("xn2T", [P, NT * P])
        wq = [sb("wq_hi", [P, INNER], F32R), sb("wq_lo", [P, INNER], F32R)]
        wkv = [sb("wkv_hi", [P, 2 * INNER], F32R), sb("wkv_lo", [P, 2 * INNER], F32R)]
        wo = [sb("wo_hi", [P, PAIRS, DIM], F32R), sb("wo_lo", [P, PAIRS, DIM], F32R)]
        sgu = [sb("sgu_hi", [P, 2 * I], F32R), sb("sgu_lo", [P, 2 * I], F32R)]
        sd = [sb("sd_hi", [P, 2, DIM], F32R), sb("sd_lo", [P, 2, DIM], F32R)]
        egu = [sb("egu_hi", [P, E, 2 * I], F32R), sb("egu_lo", [P, E, 2 * I], F32R)]
        ed = [sb("ed_hi", [P, E, 2 * DIM], F32R), sb("ed_lo", [P, E, 2 * DIM], F32R)]
        ident = sb("ident", [P, P])
        tri = sb("tri", [P, P], BF16)
        ones = sb("ones", [P, P], BF16)
        bias = sb("bias", [P, KS])
        kdim = sb("kdim", [P, 1])
        unull = sb("unull", [96, DIM], F32R)
        wts = sb("wts", [P, NT, TOPK])
        slot = sb("slot", [P, NT, TOPK], I32)
        tile_expert = sb("tile_expert", [P, SLOT_TILES], I32)
        mhalf = sb("mhalf", [P, 64])
        rslope = sb("rslope", [P, HEADS])
        g_col, b_col = sb("g_col", [P, 1]), sb("b_col", [P, 1])

        arena_a = sb("arena_a", [P, HEADS * K1 + TB * INNER + PAIRS * SEQ])
        x_all, xc, xn1, sq0 = (arena_a[:, i * NT * P:(i + 1) * NT * P].rearrange("p (t d) -> p t d", d=DIM)
                               for i in range(4))
        kT = arena_a[:, 0:HEADS * K1].rearrange("p (h k) -> p h k", k=K1)
        v = arena_a[:, HEADS * K1:HEADS * K1 + TB * INNER].rearrange("p (t d) -> p t d", d=INNER)
        qT = arena_a[:, HEADS * K1 + TB * INNER:HEADS * K1 + TB * INNER + PAIRS * SEQ].rearrange("p (c q) -> p c q", q=SEQ)
        arena_b = sb("arena_b", [P, 11008])
        at = [0]

        def carve(n):
            at[0] += n
            return arena_b[:, at[0] - n:at[0]]

        raw_gu = carve(4 * E * P).rearrange("p (w g d) -> p w g d", w=2, d=DIM)
        raw_d = carve(E * I).rearrange("p (e i) -> p e i", i=I)
        raw_sgu = carve(4 * P).rearrange("p (w c d) -> p w c d", w=2, d=DIM)
        raw_sd = carve(I)
        raw_w = carve(3 * INNER)
        raw_o = carve(PAIRS * DIM).rearrange("p (c d) -> p c d", d=DIM)
        assert at[0] <= 11008
        at[0] = 0
        mth, mga, mh = ([carve(I) for _ in range(2)] for _ in range(3))
        at[0] = 0
        ktok = [carve(INNER) for _ in range(2)]
        qtok = [carve(INNER) for _ in range(2)]
        sqb = [carve(INNER) for _ in range(2)]
        sim = [carve(KS) for _ in range(2)]
        prob = [carve(2 * KS).rearrange("p (h k) -> p h k", k=KS) for _ in range(3)]
        hs, ath, th = (arena_b[:, at[0] - 6 * KS + i * 2 * I:at[0] - 6 * KS + (i + 1) * 2 * I] for i in range(3))
        xres = carve(TB * DIM).rearrange("p (t d) -> p t d", d=DIM)
        yg = carve(TB * TOPK * DIM).rearrange("p (t c d) -> p t c d", c=TOPK, d=DIM)
        z0, z1, z2 = (carve(TB * DIM).rearrange("p (t d) -> p t d", d=DIM) for _ in range(3))
        assert at[0] <= 11008
        probT = [sb(f"probT{i}", [P, 3 * P]) for i in range(2)]

        arena_r = sb("arena_r", [P, 3072], F32R)
        rt = [0]

        def carve_r(n):
            rt[0] += n
            return arena_r[:, rt[0] - n:rt[0]]

        mxT, mhT = ([[carve_r(n), carve_r(n)] for _ in range(2)] for n in (P, I))
        rt[0] = 0
        xs1, xs2 = ([carve_r(SEQ), carve_r(SEQ)] for _ in range(2))
        oT = [[carve_r(SEQ), carve_r(SEQ)] for _ in range(2)]
        hss = [carve_r(2 * I), carve_r(2 * I)]
        pnT = sb("pnT", [96, SEQ], F32R)
        pnull = sb("pnull", [P, TB, HEADS * NNULL])
        nmx = sb("nmx", [P, HEADS, TB])
        den = sb("den", [P, HEADS, TB])
        rden = sb("rden", [P, HEADS, TB])
        ssq = sb("ssq", [P, TB, 2, HEADS])
        ssm = sb("ssm", [P, TB, 2, HEADS])
        rqk = sb("rqk", [P, TB, 2, HEADS])
        rqs = sb("rqs", [P, TB, HEADS])
        yT = sim[0][:, 0:SEQ]
        slot_now = sb("slot_now", [P, TB, TOPK], I32)
        w_now = sb("w_now", [P, TB, TOPK])

        RX = 4
        mx_in = [sb(f"mx_in{i}", [P, DIM]) for i in range(RX)]
        my = [sb(f"my{i}", [P, DIM]) for i in range(2)]

        rw_raw, rwT = sb("rw_raw", [E, DIM]), sb("rwT", [P, E])
        rbias = sb("rbias", [P, E])
        scratch = arena_a[:, 3 * NT * P:4 * NT * P]
        at[0] = 0

        def three_d(n, m):
            at[0] += n * m
            return scratch[:, at[0] - n * m:at[0]].rearrange("p (n m) -> p n m", m=m)

        lg, lth, pr, top, place = (three_d(NT, E) for _ in range(5))
        oh, pick = ([three_d(NT, E) for _ in range(TOPK)] for _ in range(2))
        tot, incl, excl, off = (three_d(E, NT) for _ in range(4))
        cmp = three_d(SLOT_TILES, E)
        topi = sb("topi", [P, NT, 8], U32)
        topf = sb("topf", [P, NT, TOPK])
        psum2, prec = sb("psum2", [P, NT]), sb("prec", [P, NT])
        iota_e, iota_s = sb("iota_e", [P, E]), sb("iota_s", [P, SLOT_TILES])
        ohs = sb("ohs", [P, NT, E], BF16)
        seg = sb("seg", [P, E, NT])
        ntile_i = sb("ntile_i", [P, E], I32)
        ntf, ntile, tend, tstart, base = (sb(n, [P, E]) for n in ("ntf", "ntile", "tend", "tstart", "base"))
        one8 = sb("one8", [P, E])
        slotf = sb("slotf", [P, NT, TOPK])
        tef, tef2 = sb("tef", [P, SLOT_TILES]), sb("tef2", [P, SLOT_TILES])

        xsum = [sb(f"xsum{i}", [P, NT]) for i in range(2)]
        nmean = [sb(f"nmean{i}", [P, NT]) for i in range(2)]
        vsum = [sb(f"vsum{i}", [P, NT]) for i in range(2)]
        var = [sb(f"var{i}", [P, NT]) for i in range(2)]
        rstd = [sb(f"rstd{i}", [P, NT]) for i in range(2)]

        qsc, ksc = sb("qsc", [P, 1]), sb("ksc", [P, 1])
        nraw = sb("nraw", [32, 2, DH])
        nsq, nss, nsm, nr = sb("nsq", [32, DH]), sb("nss", [32, 1]), sb("nsm", [32, 1]), sb("nr", [32, 1])
        nkT = sb("nkT", [P, HEADS * NNULL])
        nk2, nv2 = sb("nk2", [32, 2, DH]), sb("nv2", [32, 2, DH])
        nvT = probT[1][:, 0:PAIRS * 36]
        zeros = probT[0][:, 0:DIM]

        S = {n: sem(n) for n in [
            "x_in", "small_in", "gu_in", "d_in", "w_in", "o_in", "zero_in",
            "consts", "poolc", "dvec", "xc1_ready", "sq_ready", "var_ready", "rstd_ready", "xn1_ready", "xn2_ready",
            "t_ps", "t_ev", "rw_ps", "rw_ev", "lg_ps", "lg_ready", "lth_ready", "ohs_ready", "rank_ps",
            "chain", "slots_ready", "scattered", "w_ps", "w_hi", "w_lo", "wraw_hi", "wraw_lo",
            "n_sm", "n_r", "n2_ready", "n_ps", "nvT_ready", "u_ps", "un_hi", "un_ready", "kdim_ready", "kt_zero", "kt_null",
            "nvz",
            "m_in", "m_xps", "m_xhi", "m_xlo", "m_gups", "m_th", "m_ga", "m_h", "m_hps", "m_hhi", "m_hlo",
            "m_yps", "m_yev", "m_out", "m_xin_free", "m_xps_free", "m_xT_free", "m_gu_free", "m_h_free",
            "m_hps_free", "m_hT_free", "m_yps_free", "m_my_free",
            "xhi", "xlo", "kps", "qps", "vps", "ksq", "red", "ssm_ready", "r_ready", "kn", "qn", "vev",
            "tps", "tev", "gups", "sh_th", "sh_a", "sh_h", "sh_hi", "sh_lo",
            "sps", "ttr", "exp", "rd", "pn0", "pn1", "ptps", "ptev_a", "ptev_d", "ops", "ohi", "olo", "oread",
            "pnc", "pnps", "pn_hi", "pn_lo", "yps", "yev", "ytps", "zc", "pvd", "fin", "stored", "res_in", "gath", "gstage", "passed", "now",
        ]}
        g = type("Sems", (), S)
        block = ctx.enter_context(nc.Block())
        m_in = [sem(f"m_in{r}") for r in range(RX)]
        m_out = [sem(f"m_out{r}") for r in range(2)]

        def bc(ap, n):
            return ap.unsqueeze(2).to_broadcast([ap.shape[0], ap.shape[1], n])

        def front(ap, n):
            return ap.unsqueeze(1).to_broadcast([ap.shape[0], n, ap.shape[1]])

        RING = 2

        def done(n, ahead=RING):
            return n + 1 + ahead

        def freed(n):
            return n + 1

        groups = [([raw_gu[:, w, 2 * e + c, :] for w in range(2) for c in range(2)],
                   [t[:, e, :] for t in egu], "gu") for e in range(E)]
        groups += [([raw_d[:, e, c * P:(c + 1) * P] for e in (e2, e2 + 1) for c in range(2)],
                    [t[:, e2:e2 + 2, :].rearrange("p e n -> p (e n)") for t in ed], "d") for e2 in range(0, E, 2)]
        groups += [([raw_sgu[:, w, c, :] for w in range(2) for c in range(2)], [t[:] for t in sgu], "d"),
                   ([raw_sd[:, c * P:(c + 1) * P] for c in range(2)],
                    [t[:].rearrange("p c d -> p (c d)") for t in sd], "d")]
        EARLY = 4

        def settled(eng):
            eng.sem_inc(g.passed, 1)

        @block.sync
        def _(sync):
            xv = a["L0_attn_x"].rearrange("b (t p) d -> p (b t) d", p=P)
            sync.dma_start(x_all, xv).then_inc(g.x_in, 16)
            for w, n in enumerate(("L0_ffn_wg", "L0_ffn_wu")):
                sync.dma_start(raw_gu[:, w], a[n].rearrange("e (c p) h -> p (e c) h", p=P)).then_inc(g.gu_in, 16)
            sync.dma_start(raw_d, a["L0_ffn_wd"].rearrange("e p i -> p e i")).then_inc(g.d_in, 16)
            for w, n in enumerate(("L0_ffn_sg_w", "L0_ffn_su_w")):
                sync.dma_start(raw_sgu[:, w], a[n].rearrange("(c p) h -> p c h", p=P)).then_inc(g.d_in, 16)
            sync.dma_start(raw_sd, a["L0_ffn_sd_w"]).then_inc(g.d_in, 16)
            sync.dma_start(raw_w[:, 0:INNER], a["L0_attn_Wq"]).then_inc(g.w_in, 16)
            sync.dma_start(raw_w[:, INNER:3 * INNER], a["L0_attn_Wkv"]).then_inc(g.w_in, 16)
            sync.dma_start(raw_o, a["L0_attn_Wout"].rearrange("(c p) d -> p c d", p=P)).then_inc(g.o_in, 16)
            sync.wait_ge(g.nvz, 1)
            zv = xg_dram.rearrange("(p r) d -> p (r d)", p=P)
            for i in range(SLOT_TILES * DIM // 1280):
                sync.dma_start(zv[:, i * 1280:(i + 1) * 1280].rearrange("p (r w) -> p r w", w=DIM),
                               zeros.unsqueeze(1).to_broadcast([P, 10, DIM])).then_inc(g.zero_in, 16)

            sync.wait_ge(g.scattered, 16 * NT * TOPK)
            with sync.Fori(0, SLOT_TILES // MU) as it:
                for st in range(MU + 3):
                    j = st
                    if j < MU:
                        n = it * MU + j
                        sync.wait_ge(g.m_xps, freed(n))
                        sync.dma_start(mx_in[j % RX][:], xg_dram[bass.ds(n * P, P), :]).then_inc(m_in[j % RX], 16)
                    j = st - 3
                    if j >= 0:
                        n = it * MU + j
                        sync.wait_ge(g.m_yev, done(n))
                        sync.dma_start(yg_dram[bass.ds(n * P, P), :], my[j % RING][:]).then_inc(m_out[j % RING], 16)

            ov = out.rearrange("b (t p) d -> b p t d", p=P)
            xb = a["L0_attn_x"].rearrange("b (t p) d -> b p t d", p=P)
            with sync.Fori(0, BATCH) as b:
                sync.wait_ge(g.fin, b + 1)
                sync.dma_start(xres, xb[bass.ds(b, 1)].rearrange("a p t d -> p (a t) d")).then_inc(g.res_in, 16)
                sync.wait_ge(g.fin, b + 2)
                sync.dma_start(ov[bass.ds(b, 1)].rearrange("a p t d -> p (a t) d"), z2).then_inc(g.stored, 16)
            sync.wait_ge(g.stored, 16 * (BATCH + 1))

        @block.gpsimd
        def _(pool):
            gp = nc.gpsimd
            gp.memset(zeros, 0.0).then_inc(g.nvz, 1)
            gp.memset(ident[:], 0.0).then_inc(g.poolc, 1)
            gp.memset(ones[:], 1.0).then_inc(g.poolc, 1)
            gp.memset(tri[:], 1.0).then_inc(g.poolc, 1)
            gp.memset(mhalf[:], -0.5).then_inc(g.poolc, 1)
            gp.memset(seg[:], 1.0).then_inc(g.poolc, 1)
            gp.memset(one8[:], 1.0).then_inc(g.poolc, 1)
            gp.memset(nvT, 0.0).then_inc(g.poolc, 1)
            for h in range(HEADS):
                gp.memset(rslope[:, h:h + 1], 1.0 / SLOPES[h]).then_inc(g.poolc, 1)
            gp.iota(iota_e[:], [[1, E]], base=0, channel_multiplier=0, allow_small_or_imprecise_dtypes=True).then_inc(g.poolc, 1)
            gp.iota(iota_s[:], [[1, SLOT_TILES]], base=0, channel_multiplier=0, allow_small_or_imprecise_dtypes=True).then_inc(g.poolc, 1)
            gp.iota(bias[:, 0:K0], [[1, K0]], base=-NNULL, channel_multiplier=-1, allow_small_or_imprecise_dtypes=True).then_inc(g.poolc, 1)
            gp.iota(bias[:, K0:KS], [[1, K1]], base=-NNULL - P, channel_multiplier=-1, allow_small_or_imprecise_dtypes=True).then_inc(g.poolc, 1)
            pool.wait_ge(g.poolc, 27)
            gp.affine_select(out=ident[:], in_=ident[:], compare_op=ALU.not_equal, fill=1.0, base=0,
                             pattern=[[-1, P]], channel_multiplier=1).then_inc(g.consts, 1)
            gp.affine_select(out=tri[:], in_=tri[:], compare_op=ALU.is_gt, fill=0.0, base=0,
                             pattern=[[1, P]], channel_multiplier=-1).then_inc(g.consts, 1)
            gp.memset(seg[:, :, 0:1], 0.0).then_inc(g.consts, 1)
            gp.affine_select(out=bias[:, 0:K0], in_=bias[:, 0:K0], compare_op=ALU.is_ge, fill=MASKED, base=NNULL,
                             pattern=[[-1, K0]], channel_multiplier=1).then_inc(g.consts, 1)
            gp.affine_select(out=bias[:, K0:KS], in_=bias[:, K0:KS], compare_op=ALU.is_ge, fill=MASKED, base=NNULL + P,
                             pattern=[[-1, K1]], channel_multiplier=1).then_inc(g.consts, 1)
            for i in range(2):
                pool.wait_ge(g.var_ready, i + 1)
                gp.tensor_tensor(rstd[i][:], var[i][:], mhalf[:, 0:NT], ALU.pow).then_inc(g.rstd_ready, 1)
            pool.wait_ge(g.wraw_hi, 3)
            gp.tensor_tensor(wq[1][:], raw_w[:, 0:INNER], wq[0][:].bitcast(F32), ALU.subtract).then_inc(g.wraw_lo, 1)
            gp.tensor_tensor(wkv[1][:], raw_w[:, INNER:3 * INNER], wkv[0][:].bitcast(F32), ALU.subtract).then_inc(g.wraw_lo, 1)
            gp.tensor_tensor(wo[1][:], raw_o, wo[0][:].bitcast(F32), ALU.subtract).then_inc(g.wraw_lo, 1)
            pool.wait_ge(g.n_sm, 1)
            gp.tensor_tensor(nr[:], nsm[:], mhalf[0:32, 0:1], ALU.pow).then_inc(g.n_r, 1)
            pool.wait_ge(g.slots_ready, 1)
            pool.wait_ge(g.zero_in, 16 * (SLOT_TILES * DIM // 1280))
            for k in range(NT):
                for c in range(TOPK):
                    pool.indirect_dma_start(xg_dram, bass.IndirectOffsetOnAxis(ap=slot[:, k, c:c + 1], axis=0),
                                            xn1[:, k, :], None).then_inc(g.scattered, 16)
            pool.wait_ge(g.scattered, 16 * NT * TOPK)
            pool.wait_ge(g.t_ev, 8)
            gp.memset(arena_a[:, 0:HEADS * K1], 0.0).then_inc(g.kt_zero, 1)
            for r in range(RING):
                pool.wait_ge(m_out[r], 16 * (SLOT_TILES // RING + 1))

            with pool.Fori(0, BATCH) as b:
                for t in range(TB):
                    pool.wait_ge(g.ssm_ready, TB * b + t + 1)
                    gp.tensor_tensor(rqk[:, t].rearrange("p w h -> p (w h)"), ssm[:, t].rearrange("p w h -> p (w h)"),
                                     mhalf[:, 0:2 * HEADS], ALU.pow).then_inc(g.gstage, 1)
                    pool.wait_ge(g.gstage, 4 * b + 2 * t + 1)
                    gp.tensor_tensor(rqs[:, t, :], rqk[:, t, 1, :], rslope[:], ALU.mult).then_inc(g.gstage, 1)
                gp.tensor_copy(slot_now[:], slot[:, bass.ds(b * TB, TB), :]).then_inc(g.now, 1)
                gp.tensor_copy(w_now[:], wts[:, bass.ds(b * TB, TB), :]).then_inc(g.now, 1)
                pool.wait_ge(g.now, 2 * b + 2)
                settled(pool)
                for t in range(TB):
                    for c in range(TOPK):
                        pool.indirect_dma_start(yg[:, t, c, :], None, yg_dram,
                                                bass.IndirectOffsetOnAxis(ap=slot_now[:, t, c:c + 1], axis=0)
                                                ).then_inc(g.gath, 16)
                for h in range(HEADS):
                    p = h // 2
                    pool.wait_ge(g.rd, HEADS * b + h + 1)
                    settled(pool)
                    gp.tensor_scalar(prob[p % 3][:, h % 2, K0:KS], prob[p % 3][:, h % 2, K0:KS], rden[:, h, 1:2], None,
                                     ALU.mult).then_inc(g.pn1, 1)
                    if h % 2:
                        pool.wait_ge(g.pn0, HEADS * b + h + 1)
                        pool.wait_ge(g.pn1, HEADS * b + h + 1)
                        settled(pool)
                        gp.tensor_copy(pnull[:, 0, 4 * p:4 * p + 4].rearrange("p (h n) -> p h n", n=2),
                                       prob[p % 3][:, :, 0:NNULL]).then_inc(g.pnc, 1)
                        gp.tensor_copy(pnull[:, 1, 4 * p:4 * p + 4].rearrange("p (h n) -> p h n", n=2),
                                       prob[p % 3][:, :, K0:K0 + NNULL]).then_inc(g.pnc, 1)

        @block.scalar
        def _(act):
            sc = nc.scalar
            for i in range(2):
                act.sem_inc(m_out[i], 16)
            col = [("L0_attn_norm_g", g_col[:]), ("L0_attn_norm_b", b_col[:])]
            col += [(f"L0_attn_{w}_scale", t[r:r + DH, :]) for w, t in (("q", qsc), ("k", ksc)) for r in (0, DH)]
            for n, t in col:
                act.dma_start(t, a[n].rearrange("(p o) -> p o", o=1)).then_inc(g.small_in, 16)
            act.dma_start(nraw[:], a["L0_attn_null_kv"].rearrange("h (n w) d -> (h n) w d", w=2)).then_inc(g.small_in, 16)
            act.dma_start(rw_raw[:], a["L0_ffn_router_w"]).then_inc(g.small_in, 16)
            act.dma_start(rbias[:], a["L0_ffn_routing_bias"].rearrange("(o e) -> o e", o=1).to_broadcast([P, E])).then_inc(g.small_in, 16)

            def split_group(n):
                srcs, dst, _ = groups[n]
                w = len(srcs) * P
                act.wait_ge(g.w_ps, n + 1)
                sc.activation(dst[0], bank[n % EARLY][:, 0:w], ACT.Copy).then_inc(g.w_hi, 1)

            act.wait_ge(g.xc1_ready, 1)
            sc.activation(sq0, xc, ACT.Square).then_inc(g.sq_ready, 1)
            for n in range(EARLY):
                split_group(n)
            act.wait_ge(g.w_in, 32)
            act.wait_ge(g.o_in, 16)
            sc.activation(wq[0][:], raw_w[:, 0:INNER], ACT.Copy).then_inc(g.wraw_hi, 1)
            sc.activation(wkv[0][:], raw_w[:, INNER:3 * INNER], ACT.Copy).then_inc(g.wraw_hi, 1)
            sc.activation(wo[0][:], raw_o, ACT.Copy).then_inc(g.wraw_hi, 1)
            act.wait_ge(g.rw_ps, 1)
            sc.activation(rwT[:], bank[7][:, 0:E], ACT.Copy).then_inc(g.rw_ev, 1)
            for i in range(4):
                act.wait_ge(g.t_ps, i + 1)
                sc.activation(xn1T[:, i * 512:(i + 1) * 512], bank[4 + i % 2][:], ACT.Copy).then_inc(g.t_ev, 1)
            act.wait_ge(g.xc1_ready, 2)
            sc.activation(sq0, xc, ACT.Square).then_inc(g.sq_ready, 1)
            act.wait_ge(g.lg_ready, 1)
            sc.activation(lth, lg, ACT.Tanh, scale=0.5).then_inc(g.lth_ready, 1)
            act.wait_ge(g.small_in, 16 * 9)
            for i in range(4):
                act.wait_ge(g.t_ps, 4 + i + 1)
                sc.activation(xn2T[:, i * 512:(i + 1) * 512], bank[4 + i % 2][:], ACT.Identity,
                              scale=g_col[:, 0:1], bias=b_col[:, 0:1]).then_inc(g.t_ev, 1)
            act.wait_ge(g.n_ps, 2)
            act.wait_ge(g.kdim_ready, 1)
            sc.activation(nkT[:], bank[7][:, 64:96], ACT.Copy, scale=kdim[:, 0:1]).then_inc(g.nvT_ready, 1)
            for r, base_p in ((0, 0), (2, DH)):
                sc.activation(nvT[base_p:base_p + DH, :].rearrange("p (q c) -> p q c", c=36)[:, :, r:r + 2],
                              bank[7][base_p:base_p + DH, 96:128].rearrange("p (q c) -> p q c", c=4)[:, :, r:r + 2],
                              ACT.Copy).then_inc(g.nvT_ready, 1)
            act.wait_ge(g.u_ps, 1)
            for r in (0, 32):
                sc.activation(unull[r:r + 32, :], bank[7][0:32, 256:256 + DIM], ACT.Copy).then_inc(g.un_hi, 1)
            for n in range(EARLY, len(groups)):
                split_group(n)

            act.sem_inc(g.m_xhi, RING)
            act.sem_inc(g.m_th, RING)
            act.sem_inc(g.m_hhi, RING)
            act.sem_inc(g.m_yev, RING)
            with act.Fori(0, SLOT_TILES // MU) as it:
                for st in range(MU + 3):
                    j = st
                    if j < MU:
                        n = it * MU + j
                        act.wait_ge(g.m_xps, done(n, RX))
                        act.wait_ge(g.m_gups, freed(n))
                        sc.activation(mxT[j % 2][0], bank[j % 2][:, 0:P], ACT.Copy).then_inc(g.m_xhi, 1)
                    j = st - 1
                    if 0 <= j < MU:
                        n = it * MU + j
                        act.wait_ge(g.m_gups, done(n))
                        act.wait_ge(g.m_ga, freed(n))
                        sc.activation(mth[j % 2], bank[2 + j % 2][:, 0:I], ACT.Tanh, scale=0.5).then_inc(g.m_th, 1)
                    j = st - 2
                    if 0 <= j < MU:
                        n = it * MU + j
                        act.wait_ge(g.m_hps, done(n))
                        act.wait_ge(g.m_yps, freed(n))
                        sc.activation(mhT[j % 2][0], bank[4 + j % 2][:, 0:I], ACT.Copy).then_inc(g.m_hhi, 1)
                    j = st - 3
                    if 0 <= j < MU:
                        n = it * MU + j
                        act.wait_ge(g.m_yps, done(n))
                        act.wait_ge(m_out[j % 2], 16 * (it * (MU // 2) + j // 2 + 1))
                        sc.activation(my[j % 2][:], bank[6 + j % 2][:, 0:DIM], ACT.Copy).then_inc(g.m_yev, 1)

            act.wait_ge(g.kt_zero, 1)
            for half in range(2):
                r = slice(half * DH, half * DH + DH)
                sc.activation(kT[r, half:HEADS:2, 0:NNULL],
                              nkT[r, :].rearrange("p (q c) -> p q c", c=4)[:, :, 2 * half:2 * half + 2],
                              ACT.Copy).then_inc(g.kt_null, 1)
            with act.Fori(0, BATCH) as b:
                for xT, xs in ((xn1T, xs1), (xn2T, xs2)):
                    sc.activation(xs[0], xT[:, bass.ds(b * SEQ, SEQ)], ACT.Copy).then_inc(g.xhi, 1)
                for t in range(TB):
                    for w, ps in ((0, g.kps), (1, g.qps)):
                        act.wait_ge(ps, TB * b + t + 1)
                        if t:
                            act.wait_ge(g.red, 4 * b + w + 1)
                        for c in range(2):
                            sc.activation(sqb[w][:, c * 512:(c + 1) * 512], bank[2 * w + c][:], ACT.Square).then_inc(g.ksq, 1)
                    act.wait_ge(g.vps, TB * b + t + 1)
                    for c in range(2):
                        sc.activation(v[:, t, c * 512:(c + 1) * 512], bank[4 + c][:], ACT.Copy).then_inc(g.vev, 1)
                for t in range(TB):
                    for q in range(4):
                        act.wait_ge(g.tps, 8 * b + 4 * t + q + 1)
                        src = bank[6 + q % 2]
                        p0 = 4 * (q % 2)
                        if q < 2:
                            for half in range(2):
                                r = slice(half * DH, half * DH + DH)
                                ins = sc.activation(kT[r, 2 * p0 + half:2 * p0 + 8:2, NNULL + t * P:NNULL + (t + 1) * P],
                                                    src[r, :].rearrange("p (q k) -> p q k", k=P), ACT.Copy,
                                                    scale=kdim[r, 0:1])
                                if half:
                                    ins.then_inc(g.tev, 1)
                        else:
                            sc.activation(qT[:, p0:p0 + 4, t * P:(t + 1) * P],
                                          src[:].rearrange("p (q k) -> p q k", k=P), ACT.Copy).then_inc(g.tev, 1)
                act.wait_ge(g.gups, b + 1)
                sc.activation(th, bank[0][:], ACT.Tanh, scale=0.5).then_inc(g.sh_th, 1)
                act.wait_ge(g.sh_h, b + 1)
                sc.activation(hss[0], hs, ACT.Copy).then_inc(g.sh_hi, 1)
                for s in range(HEADS + 5):
                    h = s
                    if h < HEADS:
                        p = h // 2
                        if h % 2 == 0 and p >= 3:
                            act.wait_ge(g.ptps, HEADS * b + 2 * (p - 3) + 2)
                            act.wait_ge(g.pnc, 2 * PAIRS * b + 2 * (p - 3) + 2)
                        act.wait_ge(g.ttr, HEADS * TB * b + TB * h + TB)
                        for t, c in ((0, slice(0, K0)), (1, slice(K0, KS))):
                            sc.activation(prob[p % 3][:, h % 2, c], sim[h % 2][:, c], ACT.Exp, scale=-1.0,
                                          bias=nmx[:, h, t:t + 1], accum_out=den[:, h, t:t + 1]).then_inc(g.exp, 1)
                    h = s - 2
                    if 0 <= h < HEADS and h % 2 == 0:
                        act.wait_ge(g.ptps, HEADS * b + h + 1)
                        if h >= 2:
                            act.wait_ge(g.pvd, HEADS * b + h - 1)
                        sc.activation(probT[h % 2][:], bank[2 + h % 2][:, 0:3 * P], ACT.Copy).then_inc(g.ptev_a, 1)
                    h = s - 4
                    if 0 <= h < HEADS and h % 2:
                        p = h // 2
                        act.wait_ge(g.pvd, HEADS * b + h + 1)
                        if p >= 2:
                            act.wait_ge(g.oread, PAIRS * b + p - 1)
                        sc.activation(oT[p % 2][0], bank[4 + p % 2][:, 0:SEQ], ACT.Copy).then_inc(g.ohi, 1)
                act.wait_ge(g.pnps, b + 1)
                for r in (0, 64):
                    sc.activation(pnT[r:r + 32, :], bank[7][0:32, 0:SEQ], ACT.Copy).then_inc(g.pn_hi, 1)
                act.wait_ge(g.yps, b + 1)
                sc.activation(yT, bank[6][:, 0:SEQ], ACT.Copy).then_inc(g.yev, 1)

        @block.vector
        def _(dve):
            ve = nc.vector
            chain = [0]

            def link(ins):
                chain[0] += 1
                ins.then_inc(g.chain, 1)
                dve.wait_ge(g.chain, chain[0])

            def split_group(n):
                srcs, dst, _ = groups[n]
                w = len(srcs) * P
                dve.wait_ge(g.w_hi, n + 1)
                ve.tensor_tensor(dst[1], bank[n % EARLY][:, 0:w], dst[0].bitcast(F32), ALU.subtract).then_inc(g.w_lo, 1)

            dve.wait_ge(g.x_in, 16)
            for i, (src, dst) in enumerate(((x_all, xn1), (xn1, x_all))):
                link(ve.reduce_sum(xsum[i][:], src, AX.X))
                link(ve.tensor_scalar(nmean[i][:], xsum[i][:], -1.0 / DIM, None, ALU.mult))
                ve.tensor_tensor(xc, src, bc(nmean[i][:], DIM), ALU.add).then_inc(g.xc1_ready, 1)
                dve.wait_ge(g.sq_ready, i + 1)
                link(ve.reduce_sum(vsum[i][:], sq0, AX.X))
                ve.tensor_scalar(var[i][:], vsum[i][:], 1.0 / DIM, LN_EPS, ALU.mult, ALU.add).then_inc(g.var_ready, 1)
                if i == 0:
                    for n in range(EARLY):
                        split_group(n)
                dve.wait_ge(g.rstd_ready, i + 1)
                dve.wait_ge(g.xc1_ready, i + 1)
                ve.tensor_tensor(dst, xc, bc(rstd[i][:], DIM), ALU.mult).then_inc(g.xn1_ready if i == 0 else g.xn2_ready, 1)
                if i == 0:
                    dve.wait_ge(g.xn1_ready, 1)
            dve.wait_ge(g.small_in, 16 * 9)
            dve.wait_ge(g.lg_ps, 1)
            ve.tensor_tensor(lg, bank[6][:, 0:NT * E].rearrange("p (t e) -> p t e", e=E), front(rbias[:], NT),
                             ALU.add).then_inc(g.lg_ready, 1)
            link(ve.tensor_tensor(nsq[:], nraw[:, 0, :], nraw[:, 0, :], ALU.mult))
            link(ve.reduce_sum(nss[:], nsq[:], AX.X))
            ve.tensor_scalar(nsm[:], nss[:], L2_EPS2, None, ALU.max).then_inc(g.n_sm, 1)
            link(ve.tensor_scalar(kdim[:], qsc[:], SIM_SCALE, None, ALU.mult))
            ve.tensor_tensor(kdim[:], kdim[:], ksc[:], ALU.mult).then_inc(g.kdim_ready, 1)
            ve.tensor_copy(nv2[:, 0, :], nraw[:, 1, :]).then_inc(g.n2_ready, 1)
            ve.tensor_copy(nv2[:, 1, :], nraw[:, 1, :]).then_inc(g.n2_ready, 1)
            dve.wait_ge(g.lth_ready, 1)
            link(ve.tensor_scalar(pr, lth, 0.5, 0.5, ALU.mult, ALU.add))
            for k in range(NT):
                last = ve.max(top[:, k, :], pr[:, k, :])
            link(last)
            for k in range(NT):
                last = ve.max_index(topi[:, k, :], top[:, k, :], pr[:, k, :])
            link(last)
            link(ve.tensor_copy(topf[:], topi[:, :, 0:TOPK]))
            ve.tensor_tensor(psum2[:], top[:, :, 0], top[:, :, 1], ALU.add)
            dve.wait_ge(g.consts, 3)
            for c in range(TOPK):
                last = ve.tensor_tensor(oh[c], front(iota_e[:], NT), bc(topf[:, :, c], E), ALU.is_equal)
            link(last)
            ve.tensor_tensor(ohs[:], oh[0], oh[1], ALU.add).then_inc(g.ohs_ready, 1)
            link(ve.reciprocal(prec[:], psum2[:]))
            link(ve.tensor_tensor(wts[:], top[:, :, 0:TOPK], bc(prec[:], TOPK), ALU.mult))
            dve.wait_ge(g.rank_ps, 1)
            link(ve.tensor_copy(tot, bank[6][:, P:2 * P].rearrange("p (t e) -> p e t", e=E)))
            link(ve.tensor_tensor_scan(incl.rearrange("p e t -> p (e t)"), seg[:].rearrange("p e t -> p (e t)"),
                                       tot.rearrange("p e t -> p (e t)"), 0.0, ALU.mult, ALU.add))
            link(ve.tensor_scalar(ntf[:], incl[:, :, NT - 1], 1.0 / P, (P - 1.0) / (2 * P), ALU.mult, ALU.add))
            link(ve.tensor_copy(ntile_i[:], ntf[:]))
            link(ve.tensor_copy(ntile[:], ntile_i[:]))
            link(ve.tensor_tensor_scan(tend[:], one8[:], ntile[:], 0.0, ALU.mult, ALU.add))
            link(ve.tensor_tensor(tstart[:], tend[:], ntile[:], ALU.subtract))
            link(ve.tensor_scalar(base[:], tstart[:], float(P), None, ALU.mult))
            link(ve.tensor_tensor(excl, incl, tot, ALU.subtract))
            link(ve.tensor_tensor(off, excl, bc(base[:], NT), ALU.add))
            link(ve.tensor_tensor(place, bank[6][:, 0:P].rearrange("p (t e) -> p t e", e=E),
                                  off.rearrange("p e t -> p t e"), ALU.add))
            for c in range(TOPK):
                link(ve.tensor_tensor(pick[c], oh[c], place, ALU.mult))
                link(ve.reduce_sum(slotf[:, :, c], pick[c], AX.X))
            ve.tensor_copy(slot[:], slotf[:]).then_inc(g.slots_ready, 1)
            link(ve.tensor_tensor(cmp, bc(iota_s[:], E), front(tstart[:], SLOT_TILES), ALU.is_ge))
            link(ve.reduce_sum(tef[:], cmp, AX.X))
            link(ve.tensor_scalar(tef2[:], tef[:], -1.0, None, ALU.add))
            ve.tensor_copy(tile_expert[:], tef2[:]).then_inc(g.slots_ready, 1)
            dve.wait_ge(g.n_r, 1)
            for i in range(2):
                ve.tensor_scalar(nk2[:, i, :], nraw[:, 0, :], nr[:, 0:1], None, ALU.mult).then_inc(g.n2_ready, 1)
            dve.wait_ge(g.un_hi, 2)
            ve.tensor_tensor(unull[64:96, :], bank[7][0:32, 256:256 + DIM], unull[0:32, :].bitcast(F32),
                             ALU.subtract).then_inc(g.un_ready, 1)
            for n in range(EARLY, len(groups)):
                split_group(n)

            dve.sem_inc(g.m_xlo, RING)
            dve.sem_inc(g.m_ga, RING)
            dve.sem_inc(g.m_h, RING)
            dve.sem_inc(g.m_hlo, RING)
            with dve.Fori(0, SLOT_TILES // MU) as it:
                for st in range(MU + 2):
                    j = st
                    if j < MU:
                        n = it * MU + j
                        dve.wait_ge(g.m_xhi, done(n))
                        dve.wait_ge(g.m_gups, freed(n))
                        ve.tensor_tensor(mxT[j % 2][1], bank[j % 2][:, 0:P], mxT[j % 2][0].bitcast(F32),
                                         ALU.subtract).then_inc(g.m_xlo, 1)
                    j = st - 1
                    if 0 <= j < MU:
                        n = it * MU + j
                        ps = bank[2 + j % 2]
                        dve.wait_ge(g.m_th, done(n))
                        ve.scalar_tensor_tensor(out=mga[j % 2], in0=mth[j % 2], scalar=1.0, in1=ps[:, 0:I],
                                                op0=ALU.add, op1=ALU.mult).then_inc(g.m_ga, 1)
                        dve.wait_ge(g.m_ga, done(n))
                        dve.wait_ge(g.m_hps, freed(n))
                        ve.scalar_tensor_tensor(out=mh[j % 2], in0=mga[j % 2], scalar=0.5, in1=ps[:, I:2 * I],
                                                op0=ALU.mult, op1=ALU.mult).then_inc(g.m_h, 1)
                    j = st - 2
                    if 0 <= j < MU:
                        n = it * MU + j
                        dve.wait_ge(g.m_hhi, done(n))
                        ve.tensor_tensor(mhT[j % 2][1], bank[4 + j % 2][:, 0:I], mhT[j % 2][0].bitcast(F32),
                                         ALU.subtract).then_inc(g.m_hlo, 1)

            dve.sem_inc(g.fin, 1)
            dve.sem_inc(g.stored, 16)
            with dve.Fori(0, BATCH) as b:
                for i, (xT, xs) in enumerate(((xn1T, xs1), (xn2T, xs2))):
                    dve.wait_ge(g.xhi, 2 * b + i + 1)
                    ve.tensor_tensor(xs[1], xT[:, bass.ds(b * SEQ, SEQ)], xs[0].bitcast(F32),
                                     ALU.subtract).then_inc(g.xlo, 1)
                for t in range(TB):
                    for w in range(2):
                        dve.wait_ge(g.ksq, 8 * b + 4 * t + 2 * w + 2)
                        ve.reduce_sum(ssq[:, t, w, :], sqb[w].rearrange("p (h d) -> p h d", d=DH), AX.X).then_inc(g.red, 1)
                    dve.wait_ge(g.red, 4 * b + 2 * t + 2)
                    ve.tensor_scalar(ssm[:, t], ssq[:, t], L2_EPS2, None, ALU.max).then_inc(g.ssm_ready, 1)
                    dve.wait_ge(g.gstage, 4 * b + 2 * t + 2)
                    for w, (dst, rr, ready) in enumerate(((ktok[t], rqk[:, t, 0, :], g.kn), (qtok[t], rqs[:, t, :], g.qn))):
                        for c in range(2):
                            ins = ve.tensor_tensor(dst[:, c * 512:(c + 1) * 512].rearrange("p (h d) -> p h d", d=DH),
                                                   bank[2 * w + c][:].rearrange("p (h d) -> p h d", d=DH),
                                                   bc(rr[:, 8 * c:8 * c + 8], DH), ALU.mult)
                        ins.then_inc(ready, 1)
                dve.wait_ge(g.sh_th, b + 1)
                ve.scalar_tensor_tensor(out=ath, in0=th, scalar=1.0, in1=bank[0][:],
                                        op0=ALU.add, op1=ALU.mult).then_inc(g.sh_a, 1)
                dve.wait_ge(g.sh_a, b + 1)
                ve.scalar_tensor_tensor(out=hs, in0=ath, scalar=0.5, in1=bank[1][:],
                                        op0=ALU.mult, op1=ALU.mult).then_inc(g.sh_h, 1)
                dve.wait_ge(g.sh_hi, b + 1)
                ve.tensor_tensor(hss[1], hs, hss[0].bitcast(F32), ALU.subtract).then_inc(g.sh_lo, 1)
                for s in range(HEADS + 5):
                    h = s
                    if h < HEADS:
                        dve.wait_ge(g.sps, HEADS * b + h + 1)
                        if h >= 2:
                            dve.wait_ge(g.exp, TB * HEADS * b + TB * (h - 2) + TB)
                        settled(dve)
                        for t, c in ((0, slice(0, K0)), (1, slice(K0, KS))):
                            ve.tensor_tensor_reduce(out=sim[h % 2][:, c], in0=bank[h % 2][:, c], in1=bias[:, c],
                                                    scale=-SLOPES[h], scalar=3e38, op0=ALU.add, op1=ALU.min,
                                                    accum_out=nmx[:, h, t:t + 1]).then_inc(g.ttr, 1)
                    h = s - 1
                    if 0 <= h < HEADS:
                        dve.wait_ge(g.exp, TB * HEADS * b + TB * h + TB)
                        ve.reciprocal(rden[:, h, :], den[:, h, :]).then_inc(g.rd, 1)
                        dve.wait_ge(g.rd, HEADS * b + h + 1)
                        pr0 = prob[h // 2 % 3][:, h % 2, 0:K0]
                        ve.tensor_scalar(pr0, pr0, rden[:, h, 0:1], None, ALU.mult).then_inc(g.pn0, 1)
                    h = s - 2
                    if 0 <= h < HEADS and h % 2:
                        dve.wait_ge(g.ptps, HEADS * b + h + 1)
                        if h >= 2:
                            dve.wait_ge(g.pvd, HEADS * b + h - 1)
                        ve.tensor_copy(probT[h % 2][:], bank[2 + h % 2][:, 0:3 * P]).then_inc(g.ptev_d, 1)
                    h = s - 4
                    if 0 <= h < HEADS and h % 2:
                        p = h // 2
                        dve.wait_ge(g.ohi, PAIRS * b + p + 1)
                        ve.tensor_tensor(oT[p % 2][1], bank[4 + p % 2][:, 0:SEQ], oT[p % 2][0].bitcast(F32),
                                         ALU.subtract).then_inc(g.olo, 1)
                dve.wait_ge(g.pn_hi, 2 * b + 2)
                ve.tensor_tensor(pnT[32:64, :], bank[7][0:32, 0:SEQ], pnT[0:32, :].bitcast(F32),
                                 ALU.subtract).then_inc(g.pn_lo, 1)
                dve.wait_ge(g.ytps, b + 1)
                dve.wait_ge(g.res_in, 16 * b + 16)
                dve.wait_ge(g.gath, 16 * TB * TOPK * (b + 1))
                dve.wait_ge(g.stored, 16 * b + 16)
                ve.tensor_tensor(z0, bank[7][:, 0:SEQ].rearrange("p (t d) -> p t d", d=DIM), xres,
                                 ALU.add).then_inc(g.zc, 1)
                for c, (src, dst) in enumerate(((z0, z1), (z1, z2))):
                    dve.wait_ge(g.zc, 2 * b + c + 1)
                    for t in range(TB):
                        ins = ve.scalar_tensor_tensor(out=dst[:, t, :], in0=yg[:, t, c, :], scalar=w_now[:, t, c:c + 1],
                                                      in1=src[:, t, :], op0=ALU.mult, op1=ALU.add)
                    ins.then_inc(g.zc if c == 0 else g.fin, 1)

        @block.tensor
        def _(pe):
            te = nc.tensor

            def three(dst, lhs, rhs, first, last):
                te.matmul(dst, lhs[0], rhs[0], start=first, stop=False)
                te.matmul(dst, lhs[1], rhs[0], start=False, stop=False)
                return te.matmul(dst, lhs[0], rhs[1], start=False, stop=last)

            def transpose_group(n):
                srcs, _, _ = groups[n]
                if n == 0:
                    pe.wait_ge(g.gu_in, 32)
                if n == E:
                    pe.wait_ge(g.d_in, 64)
                if n >= EARLY:
                    pe.wait_ge(g.w_lo, n - EARLY + 1)
                for i, src in enumerate(srcs):
                    ins = te.transpose(bank[n % EARLY][:, i * P:(i + 1) * P], src, ident[:])
                ins.then_inc(g.w_ps, 1)

            pe.wait_ge(g.consts, 5)
            for n in range(EARLY):
                transpose_group(n)
            pe.wait_ge(g.small_in, 16 * 9)
            te.transpose(bank[7][:, 0:E], rw_raw[:], ident[0:E, 0:E]).then_inc(g.rw_ps, 1)
            pe.wait_ge(g.xn1_ready, 1)
            for i in range(8):
                if i >= 2:
                    pe.wait_ge(g.t_ev, i - 1)
                if i == 4:
                    pe.wait_ge(g.rw_ev, 1)
                    pe.wait_ge(g.t_ev, 4)
                    for k in range(NT):
                        ins = te.matmul(bank[6][:, k * E:(k + 1) * E], xn1T[:, k * P:(k + 1) * P], rwT[:], start=True, stop=True)
                    ins.then_inc(g.lg_ps, 1)
                    pe.wait_ge(g.xn2_ready, 1)
                src = xn1 if i < 4 else x_all
                for j in range(4):
                    ins = te.transpose(bank[4 + i % 2][:, j * P:(j + 1) * P], src[:, 4 * (i % 4) + j, :], ident[:])
                ins.then_inc(g.t_ps, 1)
            pe.wait_ge(g.ohs_ready, 1)
            oo = ohs[:].rearrange("p t e -> p (t e)")
            te.matmul(bank[6][:, 0:P], tri[:], oo, start=True, stop=True)
            te.matmul(bank[6][:, P:2 * P], ones[:], oo, start=True, stop=True).then_inc(g.rank_ps, 1)
            pe.wait_ge(g.n2_ready, 4)
            te.transpose(bank[7][:, 64:96], nk2[:].rearrange("p a d -> p (a d)"), ident[0:32, 0:32]).then_inc(g.n_ps, 1)
            te.transpose(bank[7][:, 96:128], nv2[:].rearrange("p a d -> p (a d)"), ident[0:32, 0:32]).then_inc(g.n_ps, 1)
            pe.wait_ge(g.nvT_ready, 3)
            pe.wait_ge(g.o_in, 16)
            for p in range(PAIRS):
                ins = te.matmul(bank[7][0:32, 256:256 + DIM], nvT[:, 32 * p:32 * p + 32], raw_o[:, p, :],
                                start=p == 0, stop=p == PAIRS - 1)
            ins.then_inc(g.u_ps, 1)
            for n in range(EARLY, len(groups)):
                transpose_group(n)

            pe.wait_ge(g.w_lo, len(groups))
            pe.wait_ge(g.slots_ready, 2)
            pe.sem_inc(g.m_xps, RX)
            pe.sem_inc(g.m_gups, RING)
            pe.sem_inc(g.m_hps, RING)
            pe.sem_inc(g.m_yps, RING)
            with pe.Fori(0, SLOT_TILES // MU) as it:
                ex = {}
                for st in range(MU + 3):
                    j = st
                    if j < MU:
                        n = it * MU + j
                        pe.wait_ge(m_in[j % RX], 16 * (it * (MU // RX) + j // RX + 1))
                        pe.wait_ge(g.m_xlo, freed(n))
                        te.transpose(bank[j % 2][:, 0:P], mx_in[j % RX][:], ident[:]).then_inc(g.m_xps, 1)
                        ex[j] = pe.value_load(tile_expert[0:1, bass.ds(n, 1)], min_val=0, max_val=E - 1)
                    j = st - 1
                    if 0 <= j < MU:
                        n = it * MU + j
                        pe.wait_ge(g.m_xlo, done(n))
                        pe.wait_ge(g.m_h, freed(n))
                        w = [t[:, bass.ds(ex[j], 1), :].rearrange("p o n -> p (o n)") for t in egu]
                        three(bank[2 + j % 2][:], [mxT[j % 2][0], mxT[j % 2][1]], w, True, True).then_inc(g.m_gups, 1)
                    j = st - 2
                    if 0 <= j < MU:
                        n = it * MU + j
                        pe.wait_ge(g.m_h, done(n))
                        pe.wait_ge(g.m_hlo, freed(n))
                        for c in range(2):
                            ins = te.transpose(bank[4 + j % 2][:, c * P:(c + 1) * P], mh[j % 2][:, c * P:(c + 1) * P], ident[:])
                        ins.then_inc(g.m_hps, 1)
                    j = st - 3
                    if 0 <= j < MU:
                        n = it * MU + j
                        pe.wait_ge(g.m_hlo, done(n))
                        pe.wait_ge(g.m_yev, freed(n))
                        w = [t[:, bass.ds(ex[j], 1), :].rearrange("p o n -> p (o n)") for t in ed]
                        for c in range(2):
                            cc = slice(c * P, (c + 1) * P)
                            ins = three(bank[6 + j % 2][:, 0:DIM], [x[:, cc] for x in mhT[j % 2]], [x[:, cc] for x in w],
                                        c == 0, c == 1)
                        ins.then_inc(g.m_yps, 1)

            pe.wait_ge(g.kt_null, 2)
            pe.wait_ge(g.wraw_lo, 3)
            pe.wait_ge(g.un_ready, 1)
            pe.wait_ge(g.m_yev, SLOT_TILES + RING)
            with pe.Fori(0, BATCH) as b:
                pe.wait_ge(g.xlo, 2 * b + 2)
                for t in range(TB):
                    tt = slice(t * P, (t + 1) * P)
                    for w, (xs, wt, c0, ps) in enumerate(((xs1, wkv, 0, g.kps), (xs2, wq, 0, g.qps), (xs1, wkv, INNER, g.vps))):
                        if t:
                            pe.wait_ge((g.kn, g.qn, g.vev)[w], TB * b + 1 if w < 2 else 4 * b + 2)
                        for c in range(2):
                            cc = slice(c0 + c * 512, c0 + (c + 1) * 512)
                            ins = three(bank[2 * w + c][:], [x[:, tt] for x in xs], [x[:, cc] for x in wt], True, True)
                        ins.then_inc(ps, 1)
                for t in range(TB):
                    for q in range(4):
                        pe.wait_ge(g.kn if q < 2 else g.qn, TB * b + t + 1)
                        if t or q >= 2:
                            pe.wait_ge(g.tev, 8 * b + 4 * t + q - 1)
                        elif q == 1:
                            pe.wait_ge(g.fin, b + 1)
                        src = (ktok if q < 2 else qtok)[t]
                        for j in range(4):
                            p = 4 * (q % 2) + j
                            ins = te.transpose(bank[6 + q % 2][:, j * P:(j + 1) * P], src[:, p * P:(p + 1) * P], ident[:])
                        ins.then_inc(g.tps, 1)
                for i in range(4):
                    ins = three(bank[i // 2][:, (i % 2) * SEQ:(i % 2 + 1) * SEQ], [x[:, i * P:(i + 1) * P] for x in sgu],
                                xs1, True, True)
                ins.then_inc(g.gups, 1)
                pe.wait_ge(g.tev, 8 * b + 8)
                pe.wait_ge(g.vev, 4 * b + 4)
                for s in range(HEADS + 6):
                    h = s
                    if h < HEADS:
                        if h < 2:
                            pe.wait_ge(g.sh_h, b + 1)
                        else:
                            pe.wait_ge(g.ttr, TB * HEADS * b + TB * (h - 2) + TB)
                        te.matmul(bank[h % 2][:, 0:K0], qT[:, h // 2, 0:P], kT[:, h, 0:K0], start=True, stop=True)
                        te.matmul(bank[h % 2][:, K0:KS], qT[:, h // 2, P:SEQ], kT[:, h, :], start=True, stop=True).then_inc(g.sps, 1)
                    h = s - 3
                    if 0 <= h < HEADS:
                        pe.wait_ge(g.pn0, HEADS * b + h + 1)
                        pe.wait_ge(g.pn1, HEADS * b + h + 1)
                        if h >= 2:
                            pe.wait_ge(g.ptev_d if h % 2 else g.ptev_a, PAIRS * b + h // 2)
                        pr_h = prob[h // 2 % 3][:, h % 2, :]
                        for i, c in enumerate((NNULL, K0 + NNULL, K0 + NNULL + P)):
                            ins = te.transpose(bank[2 + h % 2][:, i * P:(i + 1) * P], pr_h[:, c:c + P], ident[:])
                        ins.then_inc(g.ptps, 1)
                    h = s - 4
                    if 0 <= h < HEADS:
                        p, r = h // 2, slice((h % 2) * DH, (h % 2 + 1) * DH)
                        pe.wait_ge(g.ptev_d if h % 2 else g.ptev_a, PAIRS * b + h // 2 + 1)
                        if h % 2 == 0 and p >= 2:
                            pe.wait_ge(g.olo, PAIRS * b + p - 1)
                        o = bank[4 + p % 2]
                        te.matmul(o[r, 0:SEQ], v[:, 0, h * DH:(h + 1) * DH], probT[h % 2][:, 0:SEQ], start=True, stop=False)
                        te.matmul(o[r, P:SEQ], v[:, 1, h * DH:(h + 1) * DH], probT[h % 2][:, SEQ:3 * P], start=False,
                                  stop=True).then_inc(g.pvd, 1)
                    if s == 6:
                        pe.wait_ge(g.sh_lo, b + 1)
                        for c in range(2):
                            three(bank[6][:, 0:SEQ], [x[:, c, :] for x in sd], [x[:, c * SEQ:(c + 1) * SEQ] for x in hss],
                                  c == 0, False)
                    h = s - 6
                    if 0 <= h < HEADS and h % 2:
                        p = h // 2
                        pe.wait_ge(g.olo, PAIRS * b + p + 1)
                        three(bank[6][:, 0:SEQ], [x[:, p, :] for x in wo], oT[p % 2], False,
                              False).then_inc(g.oread, 1)
                pe.wait_ge(g.pnc, 2 * PAIRS * (b + 1))
                for t in range(TB):
                    ins = te.transpose(bank[7][0:32, t * P:(t + 1) * P], pnull[:, t, :], ident[:])
                ins.then_inc(g.pnps, 1)
                pe.wait_ge(g.pn_lo, b + 1)
                te.matmul(bank[6][:, 0:SEQ], unull[:], pnT[:], start=False, stop=True).then_inc(g.yps, 1)
                pe.wait_ge(g.yev, b + 1)
                for t in range(TB):
                    ins = te.transpose(bank[7][:, t * P:(t + 1) * P], yT[:, t * P:(t + 1) * P], ident[:])
                ins.then_inc(g.ytps, 1)

_INS = ['L0_attn_x', 'L0_attn_norm_g', 'L0_attn_norm_b', 'L0_attn_Wq', 'L0_attn_Wkv', 'L0_attn_q_scale',
        'L0_attn_k_scale', 'L0_attn_null_kv', 'L0_attn_Wout', 'L0_ffn_sg_w', 'L0_ffn_su_w', 'L0_ffn_sd_w',
        'L0_ffn_router_w', 'L0_ffn_routing_bias', 'L0_ffn_wg', 'L0_ffn_wu', 'L0_ffn_wd']


def kernel(**inputs):
    import numpy as _np
    import concourse.bacc as _bacc
    from concourse import mybir as _mybir
    from concourse.bass_utils import run_bass_kernel_spmd as _run

    nc = _bacc.Bacc("TRN2", target_bir_lowering=False, num_devices=1)
    arrays, args = {}, {}
    for name in _INS:
        a = _np.ascontiguousarray(inputs[name])
        arrays[f"in_{name}_dram"] = a
        args[name] = nc.dram_tensor(f"in_{name}_dram", a.shape, _mybir.dt.from_np(a.dtype), kind="ExternalInput").ap()
    out = nc.dram_tensor("out_0_dram", inputs['L0_attn_x'].shape, _mybir.dt.float32, kind="ExternalOutput").ap()
    build(nc, args, out)
    r = _run(nc, [arrays], core_ids=[0])
    return r.results[0]["out_0_dram"]
```

```python
from contextlib import ExitStack

import concourse.bass as bass
from concourse import mybir

F32 = mybir.dt.float32
F32R = mybir.dt.float32r
BF16 = mybir.dt.bfloat16
I32 = mybir.dt.int32
U32 = mybir.dt.uint32
ALU = mybir.AluOpType
ACT = mybir.ActivationFunctionType
AX = mybir.AxisListType

P = 128
BATCH, SEQ, DIM = 8, 256, 128
HEADS, DH, NNULL = 16, 64, 2
INNER = HEADS * DH
E, I, TOPK = 8, 256, 2
NT = BATCH * SEQ // P
TB = SEQ // P
PAIRS = HEADS // 2
K0 = NNULL + P
K1 = NNULL + SEQ
KS = K0 + K1
SIM_SCALE = 8.0
LN_EPS = 1e-5
L2_EPS2 = 1e-24
MASKED = -1e30
SLOPES = [2.0 ** (-0.5 * (h + 1)) for h in range(HEADS)]
MU = 8
SLOT_TILES = -(-(NT * TOPK + E - 1) // MU) * MU
SLOTS = SLOT_TILES * P
TURNS = SLOT_TILES // MU
RX, RY = 8, 4


def build(nc, a, out):
    with ExitStack() as ctx:
        def sb(name, shape, dt=F32):
            return ctx.enter_context(nc.sbuf_tensor(name, shape, dt))

        def sem(name):
            return ctx.enter_context(nc.semaphore(name))

        bank = [ctx.enter_context(nc.psum_tensor(f"bank{i}", [P, 512], F32)) for i in range(8)]

        xg_dram = nc.dram_tensor("slot_x", [SLOTS, DIM], F32).ap()
        yg_dram = nc.dram_tensor("slot_y", [SLOTS, DIM], F32).ap()

        xn1T = sb("xn1T", [P, NT * P])
        xn2T = sb("xn2T", [P, NT * P])
        wq = [sb("wq_hi", [P, INNER], F32R), sb("wq_lo", [P, INNER], F32R)]
        wkv = [sb("wkv_hi", [P, 2 * INNER], F32R), sb("wkv_lo", [P, 2 * INNER], F32R)]
        wo = [sb("wo_hi", [P, PAIRS, DIM], F32R), sb("wo_lo", [P, PAIRS, DIM], F32R)]
        sgu = [sb("sgu_hi", [P, 2 * I], F32R), sb("sgu_lo", [P, 2 * I], F32R)]
        sd = [sb("sd_hi", [P, 2, DIM], F32R), sb("sd_lo", [P, 2, DIM], F32R)]
        egu = [sb("egu_hi", [P, E, 2 * I], F32R), sb("egu_lo", [P, E, 2 * I], F32R)]
        ed = [sb("ed_hi", [P, E, 2 * DIM], F32R), sb("ed_lo", [P, E, 2 * DIM], F32R)]
        ident = sb("ident", [P, P])
        tri = sb("tri", [P, P], BF16)
        ones = sb("ones", [P, P], BF16)
        bias = sb("bias", [P, KS])
        kdim = sb("kdim", [P, 1])
        unull = sb("unull", [96, DIM], F32R)
        wts = sb("wts", [P, NT, TOPK])
        slot = sb("slot", [P, NT, TOPK], I32)
        tile_expert = sb("tile_expert", [P, SLOT_TILES], I32)
        mhalf = sb("mhalf", [P, 64])
        rslope = sb("rslope", [P, HEADS])
        g_col, b_col = sb("g_col", [P, 1]), sb("b_col", [P, 1])

        arena_a = sb("arena_a", [P, HEADS * K1 + TB * INNER + PAIRS * SEQ])
        x_all, xc, xn1, sq0 = (arena_a[:, i * NT * P:(i + 1) * NT * P].rearrange("p (t d) -> p t d", d=DIM)
                               for i in range(4))
        kT = arena_a[:, 0:HEADS * K1].rearrange("p (h k) -> p h k", k=K1)
        v = arena_a[:, HEADS * K1:HEADS * K1 + TB * INNER].rearrange("p (t d) -> p t d", d=INNER)
        qT = arena_a[:, HEADS * K1 + TB * INNER:HEADS * K1 + TB * INNER + PAIRS * SEQ].rearrange("p (c q) -> p c q", q=SEQ)
        arena_b = sb("arena_b", [P, 11008])
        at = [0]

        def carve(n):
            at[0] += n
            return arena_b[:, at[0] - n:at[0]]

        raw_gu = carve(4 * E * P).rearrange("p (w g d) -> p w g d", w=2, d=DIM)
        raw_d = carve(E * I).rearrange("p (e i) -> p e i", i=I)
        raw_sgu = carve(4 * P).rearrange("p (w c d) -> p w c d", w=2, d=DIM)
        raw_sd = carve(I)
        raw_w = carve(3 * INNER)
        raw_o = carve(PAIRS * DIM).rearrange("p (c d) -> p c d", d=DIM)
        assert at[0] <= 11008
        at[0] = 0
        mth, mga, mh = ([carve(I) for _ in range(2)] for _ in range(3))
        mx_in = [carve(DIM) for _ in range(RX)]
        my = [carve(DIM) for _ in range(RY)]
        at[0] = 0
        ktok = [carve(INNER) for _ in range(2)]
        qtok = [carve(INNER) for _ in range(2)]
        sqb = [carve(INNER) for _ in range(2)]
        sim = [carve(KS) for _ in range(2)]
        prob = [carve(2 * KS).rearrange("p (h k) -> p h k", k=KS) for _ in range(3)]
        hs, ath, th = (arena_b[:, at[0] - 6 * KS + i * 2 * I:at[0] - 6 * KS + (i + 1) * 2 * I] for i in range(3))
        xres = carve(TB * DIM).rearrange("p (t d) -> p t d", d=DIM)
        yg = carve(TB * TOPK * DIM).rearrange("p (t c d) -> p t c d", c=TOPK, d=DIM)
        z0, z1, z2 = (carve(TB * DIM).rearrange("p (t d) -> p t d", d=DIM) for _ in range(3))
        assert at[0] <= 11008
        probT = [sb(f"probT{i}", [P, 3 * P]) for i in range(2)]

        arena_r = sb("arena_r", [P, 3072], F32R)
        rt = [0]

        def carve_r(n):
            rt[0] += n
            return arena_r[:, rt[0] - n:rt[0]]

        mxT, mhT = ([[carve_r(n), carve_r(n)] for _ in range(2)] for n in (P, I))
        rt[0] = 0
        xs1, xs2 = ([carve_r(SEQ), carve_r(SEQ)] for _ in range(2))
        oT = [[carve_r(SEQ), carve_r(SEQ)] for _ in range(2)]
        hss = [carve_r(2 * I), carve_r(2 * I)]
        pnT = sb("pnT", [96, SEQ], F32R)
        pnull = sb("pnull", [P, TB, HEADS * NNULL])
        nmx = sb("nmx", [P, HEADS, TB])
        den = sb("den", [P, HEADS, TB])
        rden = sb("rden", [P, HEADS, TB])
        ssq = sb("ssq", [P, TB, 2, HEADS])
        ssm = sb("ssm", [P, TB, 2, HEADS])
        rqk = sb("rqk", [P, TB, 2, HEADS])
        rqs = sb("rqs", [P, TB, HEADS])
        yT = sim[0][:, 0:SEQ]
        slot_now = sb("slot_now", [P, TB, TOPK], I32)
        w_now = sb("w_now", [P, TB, TOPK])

        rw_raw, rwT = sb("rw_raw", [E, DIM]), sb("rwT", [P, E])
        rbias = sb("rbias", [P, E])
        scratch = arena_a[:, 3 * NT * P:4 * NT * P]
        at[0] = 0

        def three_d(n, m):
            at[0] += n * m
            return scratch[:, at[0] - n * m:at[0]].rearrange("p (n m) -> p n m", m=m)

        lg, lth, pr, top, place = (three_d(NT, E) for _ in range(5))
        oh, pick = ([three_d(NT, E) for _ in range(TOPK)] for _ in range(2))
        tot, incl, excl, off = (three_d(E, NT) for _ in range(4))
        cmp = three_d(SLOT_TILES, E)
        topi = sb("topi", [P, NT, 8], U32)
        topf = sb("topf", [P, NT, TOPK])
        psum2, prec = sb("psum2", [P, NT]), sb("prec", [P, NT])
        iota_e, iota_s = sb("iota_e", [P, E]), sb("iota_s", [P, SLOT_TILES])
        ohs = sb("ohs", [P, NT, E], BF16)
        seg = sb("seg", [P, E, NT])
        ntile_i = sb("ntile_i", [P, E], I32)
        ntf, ntile, tend, tstart, base = (sb(n, [P, E]) for n in ("ntf", "ntile", "tend", "tstart", "base"))
        one8 = sb("one8", [P, E])
        slotf = sb("slotf", [P, NT, TOPK])
        tef, tef2 = sb("tef", [P, SLOT_TILES]), sb("tef2", [P, SLOT_TILES])

        xsum = [sb(f"xsum{i}", [P, NT]) for i in range(2)]
        nmean = [sb(f"nmean{i}", [P, NT]) for i in range(2)]
        vsum = [sb(f"vsum{i}", [P, NT]) for i in range(2)]
        var = [sb(f"var{i}", [P, NT]) for i in range(2)]
        rstd = [sb(f"rstd{i}", [P, NT]) for i in range(2)]

        qsc, ksc = sb("qsc", [P, 1]), sb("ksc", [P, 1])
        nraw = sb("nraw", [32, 2, DH])
        nsq, nss, nsm, nr = sb("nsq", [32, DH]), sb("nss", [32, 1]), sb("nsm", [32, 1]), sb("nr", [32, 1])
        nkT = sb("nkT", [P, HEADS * NNULL])
        nk2, nv2 = sb("nk2", [32, 2, DH]), sb("nv2", [32, 2, DH])
        nvT = probT[1][:, 0:PAIRS * 36]
        zeros = probT[0][:, 0:DIM]

        S = {n: sem(n) for n in [
            "x_in", "small_in", "gu_in", "d_in", "w_in", "o_in", "zero_in",
            "consts", "poolc", "dvec", "xc1_ready", "sq_ready", "var_ready", "rstd_ready", "xn1_ready", "xn2_ready",
            "t_ps", "t_ev", "rw_ps", "rw_ev", "lg_ps", "lg_ready", "lth_ready", "ohs_ready", "rank_ps",
            "chain", "slots_ready", "scattered", "w_ps", "w_hi", "w_lo", "wraw_hi", "wraw_lo",
            "n_sm", "n_r", "n2_ready", "n_ps", "nvT_ready", "u_ps", "un_hi", "un_ready", "kdim_ready", "kt_zero", "kt_null",
            "nvz",
            "m_xps", "m_xhi", "m_xlo", "m_gups", "m_th", "m_ga", "m_h", "m_hps", "m_hhi", "m_hlo", "m_yps", "m_yev",
            "xhi", "xlo", "kps", "qps", "vps", "ksq", "red", "ssm_ready", "r_ready", "kn", "qn", "vev",
            "tps", "tev", "gups", "sh_th", "sh_a", "sh_h", "sh_hi", "sh_lo",
            "sps", "ttr", "exp", "rd", "pn0", "pn1", "ptps", "ptev_a", "ptev_d", "ops", "ohi", "olo", "oread",
            "pnc", "pnps", "pn_hi", "pn_lo", "yps", "yev", "ytps", "zc", "pvd", "fin", "stored", "res_in", "gath", "gstage", "passed", "now",
        ]}
        g = type("Sems", (), S)
        block = ctx.enter_context(nc.Block())
        m_in = [sem(f"m_in{r}") for r in range(RX)]
        m_out = [sem(f"m_out{r}") for r in range(RY)]

        def bc(ap, n):
            return ap.unsqueeze(2).to_broadcast([ap.shape[0], ap.shape[1], n])

        def front(ap, n):
            return ap.unsqueeze(1).to_broadcast([ap.shape[0], n, ap.shape[1]])

        def staged(first, drain, steps, lag):
            return {st: st - lag for st in steps if (not first or st >= lag) and (not drain or st < lag)}

        groups = [([raw_gu[:, w, 2 * e + c, :] for w in range(2) for c in range(2)],
                   [t[:, e, :] for t in egu], "gu") for e in range(E)]
        groups += [([raw_d[:, e, c * P:(c + 1) * P] for e in (e2, e2 + 1) for c in range(2)],
                    [t[:, e2:e2 + 2, :].rearrange("p e n -> p (e n)") for t in ed], "d") for e2 in range(0, E, 2)]
        groups += [([raw_sgu[:, w, c, :] for w in range(2) for c in range(2)], [t[:] for t in sgu], "d"),
                   ([raw_sd[:, c * P:(c + 1) * P] for c in range(2)],
                    [t[:].rearrange("p c d -> p (c d)") for t in sd], "d")]
        EARLY = 4

        def settled(eng):
            eng.sem_inc(g.passed, 1)

        @block.sync
        def _(sync):
            xv = a["L0_attn_x"].rearrange("b (t p) d -> p (b t) d", p=P)
            sync.dma_start(x_all, xv).then_inc(g.x_in, 16)
            for w, n in enumerate(("L0_ffn_wg", "L0_ffn_wu")):
                sync.dma_start(raw_gu[:, w], a[n].rearrange("e (c p) h -> p (e c) h", p=P)).then_inc(g.gu_in, 16)
            sync.dma_start(raw_d, a["L0_ffn_wd"].rearrange("e p i -> p e i")).then_inc(g.d_in, 16)
            for w, n in enumerate(("L0_ffn_sg_w", "L0_ffn_su_w")):
                sync.dma_start(raw_sgu[:, w], a[n].rearrange("(c p) h -> p c h", p=P)).then_inc(g.d_in, 16)
            sync.dma_start(raw_sd, a["L0_ffn_sd_w"]).then_inc(g.d_in, 16)
            sync.dma_start(raw_w[:, 0:INNER], a["L0_attn_Wq"]).then_inc(g.w_in, 16)
            sync.dma_start(raw_w[:, INNER:3 * INNER], a["L0_attn_Wkv"]).then_inc(g.w_in, 16)
            sync.dma_start(raw_o, a["L0_attn_Wout"].rearrange("(c p) d -> p c d", p=P)).then_inc(g.o_in, 16)
            sync.wait_ge(g.nvz, 1)
            zv = xg_dram.rearrange("(p r) d -> p (r d)", p=P)
            for i in range(SLOT_TILES * DIM // 1280):
                sync.dma_start(zv[:, i * 1280:(i + 1) * 1280].rearrange("p (r w) -> p r w", w=DIM),
                               zeros.unsqueeze(1).to_broadcast([P, 10, DIM])).then_inc(g.zero_in, 16)

            sync.wait_ge(g.scattered, 16 * NT * TOPK)
            sync.wait_ge(g.w_lo, len(groups))
            def turn(it, first, drain, steps=range(MU)):
                load, store = (staged(first, drain, steps, lag) for lag in (0, 5))
                for st in steps:
                    if st in load:
                        j = load[st]
                        n = it * MU + j
                        if not first or j >= RX:
                            sync.wait_ge(g.m_xps, n - RX + 1)
                        sync.dma_start(mx_in[j % RX][:], xg_dram[bass.ds(n * P, P), :]).then_inc(m_in[j % RX], 16)
                    if st in store:
                        j = store[st]
                        n = it * MU + j
                        sync.wait_ge(g.m_yev, n + 1)
                        sync.dma_start(yg_dram[bass.ds(n * P, P), :], my[j % RY][:]).then_inc(m_out[j % RY], 16)

            turn(0, True, False)
            with sync.Fori(1, TURNS) as it:
                turn(it, False, False)
            turn(TURNS, False, True, range(5))

            ov = out.rearrange("b (t p) d -> b p t d", p=P)
            xb = a["L0_attn_x"].rearrange("b (t p) d -> b p t d", p=P)
            with sync.Fori(0, BATCH) as b:
                sync.wait_ge(g.fin, b + 1)
                sync.dma_start(xres, xb[bass.ds(b, 1)].rearrange("a p t d -> p (a t) d")).then_inc(g.res_in, 16)
                sync.wait_ge(g.fin, b + 2)
                sync.dma_start(ov[bass.ds(b, 1)].rearrange("a p t d -> p (a t) d"), z2).then_inc(g.stored, 16)
            sync.wait_ge(g.stored, 16 * (BATCH + 1))

        @block.gpsimd
        def _(pool):
            gp = nc.gpsimd
            gp.memset(zeros, 0.0).then_inc(g.nvz, 1)
            gp.memset(ident[:], 0.0).then_inc(g.poolc, 1)
            gp.memset(ones[:], 1.0).then_inc(g.poolc, 1)
            gp.memset(tri[:], 1.0).then_inc(g.poolc, 1)
            gp.memset(mhalf[:], -0.5).then_inc(g.poolc, 1)
            gp.memset(seg[:], 1.0).then_inc(g.poolc, 1)
            gp.memset(one8[:], 1.0).then_inc(g.poolc, 1)
            gp.memset(nvT, 0.0).then_inc(g.poolc, 1)
            for h in range(HEADS):
                gp.memset(rslope[:, h:h + 1], 1.0 / SLOPES[h]).then_inc(g.poolc, 1)
            gp.iota(iota_e[:], [[1, E]], base=0, channel_multiplier=0, allow_small_or_imprecise_dtypes=True).then_inc(g.poolc, 1)
            gp.iota(iota_s[:], [[1, SLOT_TILES]], base=0, channel_multiplier=0, allow_small_or_imprecise_dtypes=True).then_inc(g.poolc, 1)
            gp.iota(bias[:, 0:K0], [[1, K0]], base=-NNULL, channel_multiplier=-1, allow_small_or_imprecise_dtypes=True).then_inc(g.poolc, 1)
            gp.iota(bias[:, K0:KS], [[1, K1]], base=-NNULL - P, channel_multiplier=-1, allow_small_or_imprecise_dtypes=True).then_inc(g.poolc, 1)
            pool.wait_ge(g.poolc, 27)
            gp.affine_select(out=ident[:], in_=ident[:], compare_op=ALU.not_equal, fill=1.0, base=0,
                             pattern=[[-1, P]], channel_multiplier=1).then_inc(g.consts, 1)
            gp.affine_select(out=tri[:], in_=tri[:], compare_op=ALU.is_gt, fill=0.0, base=0,
                             pattern=[[1, P]], channel_multiplier=-1).then_inc(g.consts, 1)
            gp.memset(seg[:, :, 0:1], 0.0).then_inc(g.consts, 1)
            gp.affine_select(out=bias[:, 0:K0], in_=bias[:, 0:K0], compare_op=ALU.is_ge, fill=MASKED, base=NNULL,
                             pattern=[[-1, K0]], channel_multiplier=1).then_inc(g.consts, 1)
            gp.affine_select(out=bias[:, K0:KS], in_=bias[:, K0:KS], compare_op=ALU.is_ge, fill=MASKED, base=NNULL + P,
                             pattern=[[-1, K1]], channel_multiplier=1).then_inc(g.consts, 1)
            for i in range(2):
                pool.wait_ge(g.var_ready, i + 1)
                gp.tensor_tensor(rstd[i][:], var[i][:], mhalf[:, 0:NT], ALU.pow).then_inc(g.rstd_ready, 1)
            pool.wait_ge(g.wraw_hi, 3)
            gp.tensor_tensor(wq[1][:], raw_w[:, 0:INNER], wq[0][:].bitcast(F32), ALU.subtract).then_inc(g.wraw_lo, 1)
            gp.tensor_tensor(wkv[1][:], raw_w[:, INNER:3 * INNER], wkv[0][:].bitcast(F32), ALU.subtract).then_inc(g.wraw_lo, 1)
            gp.tensor_tensor(wo[1][:], raw_o, wo[0][:].bitcast(F32), ALU.subtract).then_inc(g.wraw_lo, 1)
            pool.wait_ge(g.n_sm, 1)
            gp.tensor_tensor(nr[:], nsm[:], mhalf[0:32, 0:1], ALU.pow).then_inc(g.n_r, 1)
            pool.wait_ge(g.slots_ready, 1)
            pool.wait_ge(g.zero_in, 16 * (SLOT_TILES * DIM // 1280))
            for k in range(NT):
                for c in range(TOPK):
                    pool.indirect_dma_start(xg_dram, bass.IndirectOffsetOnAxis(ap=slot[:, k, c:c + 1], axis=0),
                                            xn1[:, k, :], None).then_inc(g.scattered, 16)
            pool.wait_ge(g.scattered, 16 * NT * TOPK)
            pool.wait_ge(g.t_ev, 8)
            gp.memset(arena_a[:, 0:HEADS * K1], 0.0).then_inc(g.kt_zero, 1)
            for r in range(RY):
                pool.wait_ge(m_out[r], 16 * (SLOT_TILES // RY))

            with pool.Fori(0, BATCH) as b:
                for t in range(TB):
                    pool.wait_ge(g.ssm_ready, TB * b + t + 1)
                    gp.tensor_tensor(rqk[:, t].rearrange("p w h -> p (w h)"), ssm[:, t].rearrange("p w h -> p (w h)"),
                                     mhalf[:, 0:2 * HEADS], ALU.pow).then_inc(g.gstage, 1)
                    pool.wait_ge(g.gstage, 4 * b + 2 * t + 1)
                    gp.tensor_tensor(rqs[:, t, :], rqk[:, t, 1, :], rslope[:], ALU.mult).then_inc(g.gstage, 1)
                gp.tensor_copy(slot_now[:], slot[:, bass.ds(b * TB, TB), :]).then_inc(g.now, 1)
                gp.tensor_copy(w_now[:], wts[:, bass.ds(b * TB, TB), :]).then_inc(g.now, 1)
                pool.wait_ge(g.now, 2 * b + 2)
                settled(pool)
                for t in range(TB):
                    for c in range(TOPK):
                        pool.indirect_dma_start(yg[:, t, c, :], None, yg_dram,
                                                bass.IndirectOffsetOnAxis(ap=slot_now[:, t, c:c + 1], axis=0)
                                                ).then_inc(g.gath, 16)
                for h in range(HEADS):
                    p = h // 2
                    pool.wait_ge(g.rd, HEADS * b + h + 1)
                    settled(pool)
                    gp.tensor_scalar(prob[p % 3][:, h % 2, K0:KS], prob[p % 3][:, h % 2, K0:KS], rden[:, h, 1:2], None,
                                     ALU.mult).then_inc(g.pn1, 1)
                    if h % 2:
                        pool.wait_ge(g.pn0, HEADS * b + h + 1)
                        pool.wait_ge(g.pn1, HEADS * b + h + 1)
                        settled(pool)
                        gp.tensor_copy(pnull[:, 0, 4 * p:4 * p + 4].rearrange("p (h n) -> p h n", n=2),
                                       prob[p % 3][:, :, 0:NNULL]).then_inc(g.pnc, 1)
                        gp.tensor_copy(pnull[:, 1, 4 * p:4 * p + 4].rearrange("p (h n) -> p h n", n=2),
                                       prob[p % 3][:, :, K0:K0 + NNULL]).then_inc(g.pnc, 1)

        @block.scalar
        def _(act):
            sc = nc.scalar
            col = [("L0_attn_norm_g", g_col[:]), ("L0_attn_norm_b", b_col[:])]
            col += [(f"L0_attn_{w}_scale", t[r:r + DH, :]) for w, t in (("q", qsc), ("k", ksc)) for r in (0, DH)]
            for n, t in col:
                act.dma_start(t, a[n].rearrange("(p o) -> p o", o=1)).then_inc(g.small_in, 16)
            act.dma_start(nraw[:], a["L0_attn_null_kv"].rearrange("h (n w) d -> (h n) w d", w=2)).then_inc(g.small_in, 16)
            act.dma_start(rw_raw[:], a["L0_ffn_router_w"]).then_inc(g.small_in, 16)
            act.dma_start(rbias[:], a["L0_ffn_routing_bias"].rearrange("(o e) -> o e", o=1).to_broadcast([P, E])).then_inc(g.small_in, 16)

            def split_group(n):
                srcs, dst, _ = groups[n]
                w = len(srcs) * P
                act.wait_ge(g.w_ps, n + 1)
                sc.activation(dst[0], bank[n % EARLY][:, 0:w], ACT.Copy).then_inc(g.w_hi, 1)

            act.wait_ge(g.xc1_ready, 1)
            sc.activation(sq0, xc, ACT.Square).then_inc(g.sq_ready, 1)
            for n in range(EARLY):
                split_group(n)
            act.wait_ge(g.w_in, 32)
            act.wait_ge(g.o_in, 16)
            sc.activation(wq[0][:], raw_w[:, 0:INNER], ACT.Copy).then_inc(g.wraw_hi, 1)
            sc.activation(wkv[0][:], raw_w[:, INNER:3 * INNER], ACT.Copy).then_inc(g.wraw_hi, 1)
            sc.activation(wo[0][:], raw_o, ACT.Copy).then_inc(g.wraw_hi, 1)
            act.wait_ge(g.rw_ps, 1)
            sc.activation(rwT[:], bank[7][:, 0:E], ACT.Copy).then_inc(g.rw_ev, 1)
            for i in range(4):
                act.wait_ge(g.t_ps, i + 1)
                sc.activation(xn1T[:, i * 512:(i + 1) * 512], bank[4 + i % 2][:], ACT.Copy).then_inc(g.t_ev, 1)
            act.wait_ge(g.xc1_ready, 2)
            sc.activation(sq0, xc, ACT.Square).then_inc(g.sq_ready, 1)
            act.wait_ge(g.lg_ready, 1)
            sc.activation(lth, lg, ACT.Tanh, scale=0.5).then_inc(g.lth_ready, 1)
            act.wait_ge(g.small_in, 16 * 9)
            for i in range(4):
                act.wait_ge(g.t_ps, 4 + i + 1)
                sc.activation(xn2T[:, i * 512:(i + 1) * 512], bank[4 + i % 2][:], ACT.Identity,
                              scale=g_col[:, 0:1], bias=b_col[:, 0:1]).then_inc(g.t_ev, 1)
            act.wait_ge(g.n_ps, 2)
            act.wait_ge(g.kdim_ready, 1)
            sc.activation(nkT[:], bank[7][:, 64:96], ACT.Copy, scale=kdim[:, 0:1]).then_inc(g.nvT_ready, 1)
            for r, base_p in ((0, 0), (2, DH)):
                sc.activation(nvT[base_p:base_p + DH, :].rearrange("p (q c) -> p q c", c=36)[:, :, r:r + 2],
                              bank[7][base_p:base_p + DH, 96:128].rearrange("p (q c) -> p q c", c=4)[:, :, r:r + 2],
                              ACT.Copy).then_inc(g.nvT_ready, 1)
            act.wait_ge(g.u_ps, 1)
            for r in (0, 32):
                sc.activation(unull[r:r + 32, :], bank[7][0:32, 256:256 + DIM], ACT.Copy).then_inc(g.un_hi, 1)
            for n in range(EARLY, len(groups)):
                split_group(n)

            def turn(it, first, drain, steps=range(MU)):
                xs, tanh, hs_, ys = (staged(first, drain, steps, lag) for lag in range(4))
                for st in steps:
                    if st in xs:
                        j = xs[st]
                        n = it * MU + j
                        act.wait_ge(g.m_xps, n + 1)
                        if not first or j >= 2:
                            act.wait_ge(g.m_gups, n - 1)
                        sc.activation(mxT[j % 2][0], bank[j % 2][:, 0:P], ACT.Copy).then_inc(g.m_xhi, 1)
                    if st in tanh:
                        j = tanh[st]
                        n = it * MU + j
                        act.wait_ge(g.m_gups, n + 1)
                        if not first or j >= 2:
                            act.wait_ge(g.m_ga, n - 1)
                        sc.activation(mth[j % 2], bank[2 + j % 2][:, 0:I], ACT.Tanh, scale=0.5).then_inc(g.m_th, 1)
                    if st in hs_:
                        j = hs_[st]
                        n = it * MU + j
                        act.wait_ge(g.m_hps, n + 1)
                        if not first or j >= 2:
                            act.wait_ge(g.m_yps, n - 1)
                        sc.activation(mhT[j % 2][0], bank[4 + j % 2][:, 0:I], ACT.Copy).then_inc(g.m_hhi, 1)
                    if st in ys:
                        j = ys[st]
                        n = it * MU + j
                        act.wait_ge(g.m_yps, n + 1)
                        if not first or j >= RY:
                            act.wait_ge(m_out[j % RY], 16 * (it * (MU // RY) + j // RY))
                        sc.activation(my[j % RY][:], bank[6 + j % 2][:, 0:DIM], ACT.Copy).then_inc(g.m_yev, 1)

            turn(0, True, False)
            with act.Fori(1, TURNS) as it:
                turn(it, False, False)
            turn(TURNS, False, True, range(3))

            act.wait_ge(g.kt_zero, 1)
            for half in range(2):
                r = slice(half * DH, half * DH + DH)
                sc.activation(kT[r, half:HEADS:2, 0:NNULL],
                              nkT[r, :].rearrange("p (q c) -> p q c", c=4)[:, :, 2 * half:2 * half + 2],
                              ACT.Copy).then_inc(g.kt_null, 1)
            with act.Fori(0, BATCH) as b:
                for xT, xs in ((xn1T, xs1), (xn2T, xs2)):
                    sc.activation(xs[0], xT[:, bass.ds(b * SEQ, SEQ)], ACT.Copy).then_inc(g.xhi, 1)
                for t in range(TB):
                    for w, ps in ((0, g.kps), (1, g.qps)):
                        act.wait_ge(ps, TB * b + t + 1)
                        if t:
                            act.wait_ge(g.red, 4 * b + w + 1)
                        for c in range(2):
                            sc.activation(sqb[w][:, c * 512:(c + 1) * 512], bank[2 * w + c][:], ACT.Square).then_inc(g.ksq, 1)
                    act.wait_ge(g.vps, TB * b + t + 1)
                    for c in range(2):
                        sc.activation(v[:, t, c * 512:(c + 1) * 512], bank[4 + c][:], ACT.Copy).then_inc(g.vev, 1)
                for t in range(TB):
                    for q in range(4):
                        act.wait_ge(g.tps, 8 * b + 4 * t + q + 1)
                        src = bank[6 + q % 2]
                        p0 = 4 * (q % 2)
                        if q < 2:
                            for half in range(2):
                                r = slice(half * DH, half * DH + DH)
                                ins = sc.activation(kT[r, 2 * p0 + half:2 * p0 + 8:2, NNULL + t * P:NNULL + (t + 1) * P],
                                                    src[r, :].rearrange("p (q k) -> p q k", k=P), ACT.Copy,
                                                    scale=kdim[r, 0:1])
                                if half:
                                    ins.then_inc(g.tev, 1)
                        else:
                            sc.activation(qT[:, p0:p0 + 4, t * P:(t + 1) * P],
                                          src[:].rearrange("p (q k) -> p q k", k=P), ACT.Copy).then_inc(g.tev, 1)
                act.wait_ge(g.gups, b + 1)
                sc.activation(th, bank[0][:], ACT.Tanh, scale=0.5).then_inc(g.sh_th, 1)
                act.wait_ge(g.sh_h, b + 1)
                sc.activation(hss[0], hs, ACT.Copy).then_inc(g.sh_hi, 1)
                for s in range(HEADS + 5):
                    h = s
                    if h < HEADS:
                        p = h // 2
                        if h % 2 == 0 and p >= 3:
                            act.wait_ge(g.ptps, HEADS * b + 2 * (p - 3) + 2)
                            act.wait_ge(g.pnc, 2 * PAIRS * b + 2 * (p - 3) + 2)
                        act.wait_ge(g.ttr, HEADS * TB * b + TB * h + TB)
                        for t, c in ((0, slice(0, K0)), (1, slice(K0, KS))):
                            sc.activation(prob[p % 3][:, h % 2, c], sim[h % 2][:, c], ACT.Exp, scale=-1.0,
                                          bias=nmx[:, h, t:t + 1], accum_out=den[:, h, t:t + 1]).then_inc(g.exp, 1)
                    h = s - 2
                    if 0 <= h < HEADS and h % 2 == 0:
                        act.wait_ge(g.ptps, HEADS * b + h + 1)
                        if h >= 2:
                            act.wait_ge(g.pvd, HEADS * b + h - 1)
                        sc.activation(probT[h % 2][:], bank[2 + h % 2][:, 0:3 * P], ACT.Copy).then_inc(g.ptev_a, 1)
                    h = s - 4
                    if 0 <= h < HEADS and h % 2:
                        p = h // 2
                        act.wait_ge(g.pvd, HEADS * b + h + 1)
                        if p >= 2:
                            act.wait_ge(g.oread, PAIRS * b + p - 1)
                        sc.activation(oT[p % 2][0], bank[4 + p % 2][:, 0:SEQ], ACT.Copy).then_inc(g.ohi, 1)
                act.wait_ge(g.pnps, b + 1)
                for r in (0, 64):
                    sc.activation(pnT[r:r + 32, :], bank[7][0:32, 0:SEQ], ACT.Copy).then_inc(g.pn_hi, 1)
                act.wait_ge(g.yps, b + 1)
                sc.activation(yT, bank[6][:, 0:SEQ], ACT.Copy).then_inc(g.yev, 1)

        @block.vector
        def _(dve):
            ve = nc.vector
            chain = [0]

            def link(ins):
                chain[0] += 1
                ins.then_inc(g.chain, 1)
                dve.wait_ge(g.chain, chain[0])

            def split_group(n):
                srcs, dst, _ = groups[n]
                w = len(srcs) * P
                dve.wait_ge(g.w_hi, n + 1)
                ve.tensor_tensor(dst[1], bank[n % EARLY][:, 0:w], dst[0].bitcast(F32), ALU.subtract).then_inc(g.w_lo, 1)

            dve.wait_ge(g.x_in, 16)
            for i, (src, dst) in enumerate(((x_all, xn1), (xn1, x_all))):
                link(ve.reduce_sum(xsum[i][:], src, AX.X))
                link(ve.tensor_scalar(nmean[i][:], xsum[i][:], -1.0 / DIM, None, ALU.mult))
                ve.tensor_tensor(xc, src, bc(nmean[i][:], DIM), ALU.add).then_inc(g.xc1_ready, 1)
                dve.wait_ge(g.sq_ready, i + 1)
                link(ve.reduce_sum(vsum[i][:], sq0, AX.X))
                ve.tensor_scalar(var[i][:], vsum[i][:], 1.0 / DIM, LN_EPS, ALU.mult, ALU.add).then_inc(g.var_ready, 1)
                if i == 0:
                    for n in range(EARLY):
                        split_group(n)
                dve.wait_ge(g.rstd_ready, i + 1)
                dve.wait_ge(g.xc1_ready, i + 1)
                ve.tensor_tensor(dst, xc, bc(rstd[i][:], DIM), ALU.mult).then_inc(g.xn1_ready if i == 0 else g.xn2_ready, 1)
                if i == 0:
                    dve.wait_ge(g.xn1_ready, 1)
            dve.wait_ge(g.small_in, 16 * 9)
            dve.wait_ge(g.lg_ps, 1)
            ve.tensor_tensor(lg, bank[6][:, 0:NT * E].rearrange("p (t e) -> p t e", e=E), front(rbias[:], NT),
                             ALU.add).then_inc(g.lg_ready, 1)
            link(ve.tensor_tensor(nsq[:], nraw[:, 0, :], nraw[:, 0, :], ALU.mult))
            link(ve.reduce_sum(nss[:], nsq[:], AX.X))
            ve.tensor_scalar(nsm[:], nss[:], L2_EPS2, None, ALU.max).then_inc(g.n_sm, 1)
            link(ve.tensor_scalar(kdim[:], qsc[:], SIM_SCALE, None, ALU.mult))
            ve.tensor_tensor(kdim[:], kdim[:], ksc[:], ALU.mult).then_inc(g.kdim_ready, 1)
            ve.tensor_copy(nv2[:, 0, :], nraw[:, 1, :]).then_inc(g.n2_ready, 1)
            ve.tensor_copy(nv2[:, 1, :], nraw[:, 1, :]).then_inc(g.n2_ready, 1)
            dve.wait_ge(g.lth_ready, 1)
            link(ve.tensor_scalar(pr, lth, 0.5, 0.5, ALU.mult, ALU.add))
            for k in range(NT):
                last = ve.max(top[:, k, :], pr[:, k, :])
            link(last)
            for k in range(NT):
                last = ve.max_index(topi[:, k, :], top[:, k, :], pr[:, k, :])
            link(last)
            link(ve.tensor_copy(topf[:], topi[:, :, 0:TOPK]))
            ve.tensor_tensor(psum2[:], top[:, :, 0], top[:, :, 1], ALU.add)
            dve.wait_ge(g.consts, 3)
            for c in range(TOPK):
                last = ve.tensor_tensor(oh[c], front(iota_e[:], NT), bc(topf[:, :, c], E), ALU.is_equal)
            link(last)
            ve.tensor_tensor(ohs[:], oh[0], oh[1], ALU.add).then_inc(g.ohs_ready, 1)
            link(ve.reciprocal(prec[:], psum2[:]))
            link(ve.tensor_tensor(wts[:], top[:, :, 0:TOPK], bc(prec[:], TOPK), ALU.mult))
            dve.wait_ge(g.rank_ps, 1)
            link(ve.tensor_copy(tot, bank[6][:, P:2 * P].rearrange("p (t e) -> p e t", e=E)))
            link(ve.tensor_tensor_scan(incl.rearrange("p e t -> p (e t)"), seg[:].rearrange("p e t -> p (e t)"),
                                       tot.rearrange("p e t -> p (e t)"), 0.0, ALU.mult, ALU.add))
            link(ve.tensor_scalar(ntf[:], incl[:, :, NT - 1], 1.0 / P, (P - 1.0) / (2 * P), ALU.mult, ALU.add))
            link(ve.tensor_copy(ntile_i[:], ntf[:]))
            link(ve.tensor_copy(ntile[:], ntile_i[:]))
            link(ve.tensor_tensor_scan(tend[:], one8[:], ntile[:], 0.0, ALU.mult, ALU.add))
            link(ve.tensor_tensor(tstart[:], tend[:], ntile[:], ALU.subtract))
            link(ve.tensor_scalar(base[:], tstart[:], float(P), None, ALU.mult))
            link(ve.tensor_tensor(excl, incl, tot, ALU.subtract))
            link(ve.tensor_tensor(off, excl, bc(base[:], NT), ALU.add))
            link(ve.tensor_tensor(place, bank[6][:, 0:P].rearrange("p (t e) -> p t e", e=E),
                                  off.rearrange("p e t -> p t e"), ALU.add))
            for c in range(TOPK):
                link(ve.tensor_tensor(pick[c], oh[c], place, ALU.mult))
                link(ve.reduce_sum(slotf[:, :, c], pick[c], AX.X))
            ve.tensor_copy(slot[:], slotf[:]).then_inc(g.slots_ready, 1)
            link(ve.tensor_tensor(cmp, bc(iota_s[:], E), front(tstart[:], SLOT_TILES), ALU.is_ge))
            link(ve.reduce_sum(tef[:], cmp, AX.X))
            link(ve.tensor_scalar(tef2[:], tef[:], -1.0, None, ALU.add))
            ve.tensor_copy(tile_expert[:], tef2[:]).then_inc(g.slots_ready, 1)
            dve.wait_ge(g.n_r, 1)
            for i in range(2):
                ve.tensor_scalar(nk2[:, i, :], nraw[:, 0, :], nr[:, 0:1], None, ALU.mult).then_inc(g.n2_ready, 1)
            dve.wait_ge(g.un_hi, 2)
            ve.tensor_tensor(unull[64:96, :], bank[7][0:32, 256:256 + DIM], unull[0:32, :].bitcast(F32),
                             ALU.subtract).then_inc(g.un_ready, 1)
            for n in range(EARLY, len(groups)):
                split_group(n)

            def turn(it, first, drain, steps=range(MU)):
                xs, mid, hs_ = (staged(first, drain, steps, lag) for lag in range(3))
                for st in steps:
                    if st in xs:
                        j = xs[st]
                        n = it * MU + j
                        dve.wait_ge(g.m_xhi, n + 1)
                        if not first or j >= 2:
                            dve.wait_ge(g.m_gups, n - 1)
                        ve.tensor_tensor(mxT[j % 2][1], bank[j % 2][:, 0:P], mxT[j % 2][0].bitcast(F32),
                                         ALU.subtract).then_inc(g.m_xlo, 1)
                    if st in mid:
                        j = mid[st]
                        n = it * MU + j
                        ps = bank[2 + j % 2]
                        dve.wait_ge(g.m_th, n + 1)
                        ve.scalar_tensor_tensor(out=mga[j % 2], in0=mth[j % 2], scalar=1.0, in1=ps[:, 0:I],
                                                op0=ALU.add, op1=ALU.mult).then_inc(g.m_ga, 1)
                        dve.wait_ge(g.m_ga, n + 1)
                        if not first or j >= 2:
                            dve.wait_ge(g.m_hps, n - 1)
                        ve.scalar_tensor_tensor(out=mh[j % 2], in0=mga[j % 2], scalar=0.5, in1=ps[:, I:2 * I],
                                                op0=ALU.mult, op1=ALU.mult).then_inc(g.m_h, 1)
                    if st in hs_:
                        j = hs_[st]
                        n = it * MU + j
                        dve.wait_ge(g.m_hhi, n + 1)
                        ve.tensor_tensor(mhT[j % 2][1], bank[4 + j % 2][:, 0:I], mhT[j % 2][0].bitcast(F32),
                                         ALU.subtract).then_inc(g.m_hlo, 1)

            turn(0, True, False)
            with dve.Fori(1, TURNS) as it:
                turn(it, False, False)
            turn(TURNS, False, True, range(2))

            dve.sem_inc(g.fin, 1)
            dve.sem_inc(g.stored, 16)
            with dve.Fori(0, BATCH) as b:
                for i, (xT, xs) in enumerate(((xn1T, xs1), (xn2T, xs2))):
                    dve.wait_ge(g.xhi, 2 * b + i + 1)
                    ve.tensor_tensor(xs[1], xT[:, bass.ds(b * SEQ, SEQ)], xs[0].bitcast(F32),
                                     ALU.subtract).then_inc(g.xlo, 1)
                for t in range(TB):
                    for w in range(2):
                        dve.wait_ge(g.ksq, 8 * b + 4 * t + 2 * w + 2)
                        ve.reduce_sum(ssq[:, t, w, :], sqb[w].rearrange("p (h d) -> p h d", d=DH), AX.X).then_inc(g.red, 1)
                    dve.wait_ge(g.red, 4 * b + 2 * t + 2)
                    ve.tensor_scalar(ssm[:, t], ssq[:, t], L2_EPS2, None, ALU.max).then_inc(g.ssm_ready, 1)
                    dve.wait_ge(g.gstage, 4 * b + 2 * t + 2)
                    for w, (dst, rr, ready) in enumerate(((ktok[t], rqk[:, t, 0, :], g.kn), (qtok[t], rqs[:, t, :], g.qn))):
                        for c in range(2):
                            ins = ve.tensor_tensor(dst[:, c * 512:(c + 1) * 512].rearrange("p (h d) -> p h d", d=DH),
                                                   bank[2 * w + c][:].rearrange("p (h d) -> p h d", d=DH),
                                                   bc(rr[:, 8 * c:8 * c + 8], DH), ALU.mult)
                        ins.then_inc(ready, 1)
                dve.wait_ge(g.sh_th, b + 1)
                ve.scalar_tensor_tensor(out=ath, in0=th, scalar=1.0, in1=bank[0][:],
                                        op0=ALU.add, op1=ALU.mult).then_inc(g.sh_a, 1)
                dve.wait_ge(g.sh_a, b + 1)
                ve.scalar_tensor_tensor(out=hs, in0=ath, scalar=0.5, in1=bank[1][:],
                                        op0=ALU.mult, op1=ALU.mult).then_inc(g.sh_h, 1)
                dve.wait_ge(g.sh_hi, b + 1)
                ve.tensor_tensor(hss[1], hs, hss[0].bitcast(F32), ALU.subtract).then_inc(g.sh_lo, 1)
                for s in range(HEADS + 5):
                    h = s
                    if h < HEADS:
                        dve.wait_ge(g.sps, HEADS * b + h + 1)
                        if h >= 2:
                            dve.wait_ge(g.exp, TB * HEADS * b + TB * (h - 2) + TB)
                        settled(dve)
                        for t, c in ((0, slice(0, K0)), (1, slice(K0, KS))):
                            ve.tensor_tensor_reduce(out=sim[h % 2][:, c], in0=bank[h % 2][:, c], in1=bias[:, c],
                                                    scale=-SLOPES[h], scalar=3e38, op0=ALU.add, op1=ALU.min,
                                                    accum_out=nmx[:, h, t:t + 1]).then_inc(g.ttr, 1)
                    h = s - 1
                    if 0 <= h < HEADS:
                        dve.wait_ge(g.exp, TB * HEADS * b + TB * h + TB)
                        ve.reciprocal(rden[:, h, :], den[:, h, :]).then_inc(g.rd, 1)
                        dve.wait_ge(g.rd, HEADS * b + h + 1)
                        pr0 = prob[h // 2 % 3][:, h % 2, 0:K0]
                        ve.tensor_scalar(pr0, pr0, rden[:, h, 0:1], None, ALU.mult).then_inc(g.pn0, 1)
                    h = s - 2
                    if 0 <= h < HEADS and h % 2:
                        dve.wait_ge(g.ptps, HEADS * b + h + 1)
                        if h >= 2:
                            dve.wait_ge(g.pvd, HEADS * b + h - 1)
                        ve.tensor_copy(probT[h % 2][:], bank[2 + h % 2][:, 0:3 * P]).then_inc(g.ptev_d, 1)
                    h = s - 4
                    if 0 <= h < HEADS and h % 2:
                        p = h // 2
                        dve.wait_ge(g.ohi, PAIRS * b + p + 1)
                        ve.tensor_tensor(oT[p % 2][1], bank[4 + p % 2][:, 0:SEQ], oT[p % 2][0].bitcast(F32),
                                         ALU.subtract).then_inc(g.olo, 1)
                dve.wait_ge(g.pn_hi, 2 * b + 2)
                ve.tensor_tensor(pnT[32:64, :], bank[7][0:32, 0:SEQ], pnT[0:32, :].bitcast(F32),
                                 ALU.subtract).then_inc(g.pn_lo, 1)
                dve.wait_ge(g.ytps, b + 1)
                dve.wait_ge(g.res_in, 16 * b + 16)
                dve.wait_ge(g.gath, 16 * TB * TOPK * (b + 1))
                dve.wait_ge(g.stored, 16 * b + 16)
                ve.tensor_tensor(z0, bank[7][:, 0:SEQ].rearrange("p (t d) -> p t d", d=DIM), xres,
                                 ALU.add).then_inc(g.zc, 1)
                for c, (src, dst) in enumerate(((z0, z1), (z1, z2))):
                    dve.wait_ge(g.zc, 2 * b + c + 1)
                    for t in range(TB):
                        ins = ve.scalar_tensor_tensor(out=dst[:, t, :], in0=yg[:, t, c, :], scalar=w_now[:, t, c:c + 1],
                                                      in1=src[:, t, :], op0=ALU.mult, op1=ALU.add)
                    ins.then_inc(g.zc if c == 0 else g.fin, 1)

        @block.tensor
        def _(pe):
            te = nc.tensor

            def three(dst, lhs, rhs, first, last):
                te.matmul(dst, lhs[0], rhs[0], start=first, stop=False)
                te.matmul(dst, lhs[1], rhs[0], start=False, stop=False)
                return te.matmul(dst, lhs[0], rhs[1], start=False, stop=last)

            def transpose_group(n):
                srcs, _, _ = groups[n]
                if n == 0:
                    pe.wait_ge(g.gu_in, 32)
                if n == E:
                    pe.wait_ge(g.d_in, 64)
                if n >= EARLY:
                    pe.wait_ge(g.w_lo, n - EARLY + 1)
                for i, src in enumerate(srcs):
                    ins = te.transpose(bank[n % EARLY][:, i * P:(i + 1) * P], src, ident[:])
                ins.then_inc(g.w_ps, 1)

            pe.wait_ge(g.consts, 5)
            for n in range(EARLY):
                transpose_group(n)
            pe.wait_ge(g.small_in, 16 * 9)
            te.transpose(bank[7][:, 0:E], rw_raw[:], ident[0:E, 0:E]).then_inc(g.rw_ps, 1)
            pe.wait_ge(g.xn1_ready, 1)
            for i in range(8):
                if i >= 2:
                    pe.wait_ge(g.t_ev, i - 1)
                if i == 4:
                    pe.wait_ge(g.rw_ev, 1)
                    pe.wait_ge(g.t_ev, 4)
                    for k in range(NT):
                        ins = te.matmul(bank[6][:, k * E:(k + 1) * E], xn1T[:, k * P:(k + 1) * P], rwT[:], start=True, stop=True)
                    ins.then_inc(g.lg_ps, 1)
                    pe.wait_ge(g.xn2_ready, 1)
                src = xn1 if i < 4 else x_all
                for j in range(4):
                    ins = te.transpose(bank[4 + i % 2][:, j * P:(j + 1) * P], src[:, 4 * (i % 4) + j, :], ident[:])
                ins.then_inc(g.t_ps, 1)
            pe.wait_ge(g.ohs_ready, 1)
            oo = ohs[:].rearrange("p t e -> p (t e)")
            te.matmul(bank[6][:, 0:P], tri[:], oo, start=True, stop=True)
            te.matmul(bank[6][:, P:2 * P], ones[:], oo, start=True, stop=True).then_inc(g.rank_ps, 1)
            pe.wait_ge(g.n2_ready, 4)
            te.transpose(bank[7][:, 64:96], nk2[:].rearrange("p a d -> p (a d)"), ident[0:32, 0:32]).then_inc(g.n_ps, 1)
            te.transpose(bank[7][:, 96:128], nv2[:].rearrange("p a d -> p (a d)"), ident[0:32, 0:32]).then_inc(g.n_ps, 1)
            pe.wait_ge(g.nvT_ready, 3)
            pe.wait_ge(g.o_in, 16)
            for p in range(PAIRS):
                ins = te.matmul(bank[7][0:32, 256:256 + DIM], nvT[:, 32 * p:32 * p + 32], raw_o[:, p, :],
                                start=p == 0, stop=p == PAIRS - 1)
            ins.then_inc(g.u_ps, 1)
            for n in range(EARLY, len(groups)):
                transpose_group(n)

            pe.wait_ge(g.w_lo, len(groups))
            pe.wait_ge(g.slots_ready, 2)

            def expert_of(n):
                return pe.value_load(tile_expert[0:1, bass.ds(n, 1)], min_val=0, max_val=E - 1)

            def turn(it, first, drain, steps=range(MU)):
                xs, gu, ht, down = (staged(first, drain, steps, lag) for lag in range(4))
                for st in steps:
                    if st in xs:
                        j = xs[st]
                        n = it * MU + j
                        pe.wait_ge(m_in[j % RX], 16 * (it * (MU // RX) + j // RX + 1))
                        if not first or j >= 2:
                            pe.wait_ge(g.m_xlo, n - 1)
                        te.transpose(bank[j % 2][:, 0:P], mx_in[j % RX][:], ident[:]).then_inc(g.m_xps, 1)
                    if st in gu:
                        j = gu[st]
                        n = it * MU + j
                        e = expert_of(n)
                        pe.wait_ge(g.m_xlo, n + 1)
                        if not first or j >= 2:
                            pe.wait_ge(g.m_h, n - 1)
                        w = [t[:, bass.ds(e, 1), :].rearrange("p o n -> p (o n)") for t in egu]
                        three(bank[2 + j % 2][:], [mxT[j % 2][0], mxT[j % 2][1]], w, True, True).then_inc(g.m_gups, 1)
                    if st in ht:
                        j = ht[st]
                        n = it * MU + j
                        pe.wait_ge(g.m_h, n + 1)
                        if not first or j >= 2:
                            pe.wait_ge(g.m_hlo, n - 1)
                        for c in range(2):
                            ins = te.transpose(bank[4 + j % 2][:, c * P:(c + 1) * P], mh[j % 2][:, c * P:(c + 1) * P], ident[:])
                        ins.then_inc(g.m_hps, 1)
                    if st in down:
                        j = down[st]
                        n = it * MU + j
                        e = expert_of(n)
                        pe.wait_ge(g.m_hlo, n + 1)
                        if not first or j >= 2:
                            pe.wait_ge(g.m_yev, n - 1)
                        w = [t[:, bass.ds(e, 1), :].rearrange("p o n -> p (o n)") for t in ed]
                        for c in range(2):
                            cc = slice(c * P, (c + 1) * P)
                            ins = three(bank[6 + j % 2][:, 0:DIM], [x[:, cc] for x in mhT[j % 2]], [x[:, cc] for x in w],
                                        c == 0, c == 1)
                        ins.then_inc(g.m_yps, 1)

            turn(0, True, False)
            with pe.Fori(1, TURNS) as it:
                turn(it, False, False)
            turn(TURNS, False, True, range(3))

            pe.wait_ge(g.kt_null, 2)
            pe.wait_ge(g.wraw_lo, 3)
            pe.wait_ge(g.un_ready, 1)
            pe.wait_ge(g.m_yev, SLOT_TILES)
            with pe.Fori(0, BATCH) as b:
                pe.wait_ge(g.xlo, 2 * b + 2)
                for t in range(TB):
                    tt = slice(t * P, (t + 1) * P)
                    for w, (xs, wt, c0, ps) in enumerate(((xs1, wkv, 0, g.kps), (xs2, wq, 0, g.qps), (xs1, wkv, INNER, g.vps))):
                        if t:
                            pe.wait_ge((g.kn, g.qn, g.vev)[w], TB * b + 1 if w < 2 else 4 * b + 2)
                        for c in range(2):
                            cc = slice(c0 + c * 512, c0 + (c + 1) * 512)
                            ins = three(bank[2 * w + c][:], [x[:, tt] for x in xs], [x[:, cc] for x in wt], True, True)
                        ins.then_inc(ps, 1)
                for t in range(TB):
                    for q in range(4):
                        pe.wait_ge(g.kn if q < 2 else g.qn, TB * b + t + 1)
                        if t or q >= 2:
                            pe.wait_ge(g.tev, 8 * b + 4 * t + q - 1)
                        elif q == 1:
                            pe.wait_ge(g.fin, b + 1)
                        src = (ktok if q < 2 else qtok)[t]
                        for j in range(4):
                            p = 4 * (q % 2) + j
                            ins = te.transpose(bank[6 + q % 2][:, j * P:(j + 1) * P], src[:, p * P:(p + 1) * P], ident[:])
                        ins.then_inc(g.tps, 1)
                for i in range(4):
                    ins = three(bank[i // 2][:, (i % 2) * SEQ:(i % 2 + 1) * SEQ], [x[:, i * P:(i + 1) * P] for x in sgu],
                                xs1, True, True)
                ins.then_inc(g.gups, 1)
                pe.wait_ge(g.tev, 8 * b + 8)
                pe.wait_ge(g.vev, 4 * b + 4)
                for s in range(HEADS + 6):
                    h = s
                    if h < HEADS:
                        if h < 2:
                            pe.wait_ge(g.sh_h, b + 1)
                        else:
                            pe.wait_ge(g.ttr, TB * HEADS * b + TB * (h - 2) + TB)
                        te.matmul(bank[h % 2][:, 0:K0], qT[:, h // 2, 0:P], kT[:, h, 0:K0], start=True, stop=True)
                        te.matmul(bank[h % 2][:, K0:KS], qT[:, h // 2, P:SEQ], kT[:, h, :], start=True, stop=True).then_inc(g.sps, 1)
                    h = s - 3
                    if 0 <= h < HEADS:
                        pe.wait_ge(g.pn0, HEADS * b + h + 1)
                        pe.wait_ge(g.pn1, HEADS * b + h + 1)
                        if h >= 2:
                            pe.wait_ge(g.ptev_d if h % 2 else g.ptev_a, PAIRS * b + h // 2)
                        pr_h = prob[h // 2 % 3][:, h % 2, :]
                        for i, c in enumerate((NNULL, K0 + NNULL, K0 + NNULL + P)):
                            ins = te.transpose(bank[2 + h % 2][:, i * P:(i + 1) * P], pr_h[:, c:c + P], ident[:])
                        ins.then_inc(g.ptps, 1)
                    h = s - 4
                    if 0 <= h < HEADS:
                        p, r = h // 2, slice((h % 2) * DH, (h % 2 + 1) * DH)
                        pe.wait_ge(g.ptev_d if h % 2 else g.ptev_a, PAIRS * b + h // 2 + 1)
                        if h % 2 == 0 and p >= 2:
                            pe.wait_ge(g.olo, PAIRS * b + p - 1)
                        o = bank[4 + p % 2]
                        te.matmul(o[r, 0:SEQ], v[:, 0, h * DH:(h + 1) * DH], probT[h % 2][:, 0:SEQ], start=True, stop=False)
                        te.matmul(o[r, P:SEQ], v[:, 1, h * DH:(h + 1) * DH], probT[h % 2][:, SEQ:3 * P], start=False,
                                  stop=True).then_inc(g.pvd, 1)
                    if s == 6:
                        pe.wait_ge(g.sh_lo, b + 1)
                        for c in range(2):
                            three(bank[6][:, 0:SEQ], [x[:, c, :] for x in sd], [x[:, c * SEQ:(c + 1) * SEQ] for x in hss],
                                  c == 0, False)
                    h = s - 6
                    if 0 <= h < HEADS and h % 2:
                        p = h // 2
                        pe.wait_ge(g.olo, PAIRS * b + p + 1)
                        three(bank[6][:, 0:SEQ], [x[:, p, :] for x in wo], oT[p % 2], False,
                              False).then_inc(g.oread, 1)
                pe.wait_ge(g.pnc, 2 * PAIRS * (b + 1))
                for t in range(TB):
                    ins = te.transpose(bank[7][0:32, t * P:(t + 1) * P], pnull[:, t, :], ident[:])
                ins.then_inc(g.pnps, 1)
                pe.wait_ge(g.pn_lo, b + 1)
                te.matmul(bank[6][:, 0:SEQ], unull[:], pnT[:], start=False, stop=True).then_inc(g.yps, 1)
                pe.wait_ge(g.yev, b + 1)
                for t in range(TB):
                    ins = te.transpose(bank[7][:, t * P:(t + 1) * P], yT[:, t * P:(t + 1) * P], ident[:])
                ins.then_inc(g.ytps, 1)

_INS = ['L0_attn_x', 'L0_attn_norm_g', 'L0_attn_norm_b', 'L0_attn_Wq', 'L0_attn_Wkv', 'L0_attn_q_scale',
        'L0_attn_k_scale', 'L0_attn_null_kv', 'L0_attn_Wout', 'L0_ffn_sg_w', 'L0_ffn_su_w', 'L0_ffn_sd_w',
        'L0_ffn_router_w', 'L0_ffn_routing_bias', 'L0_ffn_wg', 'L0_ffn_wu', 'L0_ffn_wd']


def kernel(**inputs):
    import numpy as _np
    import concourse.bacc as _bacc
    from concourse import mybir as _mybir
    from concourse.bass_utils import run_bass_kernel_spmd as _run

    nc = _bacc.Bacc("TRN2", target_bir_lowering=False, num_devices=1)
    arrays, args = {}, {}
    for name in _INS:
        a = _np.ascontiguousarray(inputs[name])
        arrays[f"in_{name}_dram"] = a
        args[name] = nc.dram_tensor(f"in_{name}_dram", a.shape, _mybir.dt.from_np(a.dtype), kind="ExternalInput").ap()
    out = nc.dram_tensor("out_0_dram", inputs['L0_attn_x'].shape, _mybir.dt.float32, kind="ExternalOutput").ap()
    build(nc, args, out)
    r = _run(nc, [arrays], core_ids=[0])
    return r.results[0]["out_0_dram"]
```

```python
from contextlib import ExitStack

import concourse.bass as bass
from concourse import mybir

F32 = mybir.dt.float32
F32R = mybir.dt.float32r
BF16 = mybir.dt.bfloat16
I32 = mybir.dt.int32
U32 = mybir.dt.uint32
ALU = mybir.AluOpType
ACT = mybir.ActivationFunctionType
AX = mybir.AxisListType

P = 128
BATCH, SEQ, DIM = 8, 256, 128
HEADS, DH, NNULL = 16, 64, 2
INNER = HEADS * DH
E, I, TOPK = 8, 256, 2
NT = BATCH * SEQ // P
TB = SEQ // P
PAIRS = HEADS // 2
K0 = NNULL + P
K1 = NNULL + SEQ
KS = K0 + K1
SIM_SCALE = 8.0
LN_EPS = 1e-5
L2_EPS2 = 1e-24
MASKED = -1e30
SLOPES = [2.0 ** (-0.5 * (h + 1)) for h in range(HEADS)]
MU = 8
SLOT_TILES = -(-(NT * TOPK + E - 1) // MU) * MU
SLOTS = SLOT_TILES * P
AHEAD = 5
DRAIN = 9
TURNS = SLOT_TILES // MU
RX, RY, RH = 8, 4, 4

def build(nc, a, out):
    with ExitStack() as ctx:
        def sb(name, shape, dt=F32):
            return ctx.enter_context(nc.sbuf_tensor(name, shape, dt))

        def sem(name):
            return ctx.enter_context(nc.semaphore(name))

        bank = [ctx.enter_context(nc.psum_tensor(f"bank{i}", [P, 512], F32)) for i in range(8)]

        xg_dram = nc.dram_tensor("slot_x", [SLOTS, DIM], F32).ap()
        yg_dram = nc.dram_tensor("slot_y", [SLOTS, DIM], F32).ap()

        xn1T = sb("xn1T", [P, NT * P])
        xn2T = sb("xn2T", [P, NT * P])
        wq = [sb("wq_hi", [P, INNER], F32R), sb("wq_lo", [P, INNER], F32R)]
        wkv = [sb("wkv_hi", [P, 2 * INNER], F32R), sb("wkv_lo", [P, 2 * INNER], F32R)]
        wo = [sb("wo_hi", [P, PAIRS, DIM], F32R), sb("wo_lo", [P, PAIRS, DIM], F32R)]
        sgu = [sb("sgu_hi", [P, 2 * I], F32R), sb("sgu_lo", [P, 2 * I], F32R)]
        sd = [sb("sd_hi", [P, 2, DIM], F32R), sb("sd_lo", [P, 2, DIM], F32R)]
        egu = [sb("egu_hi", [P, E, 2 * I], F32R), sb("egu_lo", [P, E, 2 * I], F32R)]
        ed = [sb("ed_hi", [P, E, 2 * DIM], F32R), sb("ed_lo", [P, E, 2 * DIM], F32R)]
        ident = sb("ident", [P, P])
        tri = sb("tri", [P, P], BF16)
        ones = sb("ones", [P, P], BF16)
        bias = sb("bias", [P, KS])
        kdim = sb("kdim", [P, 1])
        unull = sb("unull", [96, DIM], F32R)
        wts = sb("wts", [P, NT, TOPK])
        slot = sb("slot", [P, NT, TOPK], I32)
        tile_expert = sb("tile_expert", [P, SLOT_TILES], I32)
        mhalf = sb("mhalf", [P, 64])
        rslope = sb("rslope", [P, HEADS])
        g_col, b_col = sb("g_col", [P, 1]), sb("b_col", [P, 1])

        arena_a = sb("arena_a", [P, HEADS * K1 + TB * INNER + PAIRS * SEQ])
        free_at = [0, NT * P, HEADS * K1, HEADS * K1 + NT * P]
        x_all, xc, sq0, xn1 = (arena_a[:, i:i + NT * P].rearrange("p (t d) -> p t d", d=DIM) for i in free_at)
        kT = arena_a[:, 0:HEADS * K1].rearrange("p (h k) -> p h k", k=K1)
        qT = arena_a[:, HEADS * K1:HEADS * K1 + PAIRS * SEQ].rearrange("p (c q) -> p c q", q=SEQ)
        v = arena_a[:, HEADS * K1 + PAIRS * SEQ:HEADS * K1 + PAIRS * SEQ + TB * INNER].rearrange("p (t d) -> p t d", d=INNER)
        arena_b = sb("arena_b", [P, 11008])
        at = [0]

        def carve(n):
            at[0] += n
            return arena_b[:, at[0] - n:at[0]]

        raw_gu = carve(4 * E * P).rearrange("p (w g d) -> p w g d", w=2, d=DIM)
        raw_d = carve(E * I).rearrange("p (e i) -> p e i", i=I)
        raw_sgu = carve(4 * P).rearrange("p (w c d) -> p w c d", w=2, d=DIM)
        raw_sd = carve(I)
        raw_w = carve(3 * INNER)
        raw_o = carve(PAIRS * DIM).rearrange("p (c d) -> p c d", d=DIM)
        assert at[0] <= 11008
        at[0] = 0
        ktok = [carve(INNER) for _ in range(2)]
        qtok = [carve(INNER) for _ in range(2)]
        sqb = [carve(512) for _ in range(2)]
        loop_from = at[0]
        mth, mga = ([carve(I) for _ in range(2)] for _ in range(2))
        mh = [carve(I) for _ in range(RH)]
        mx_in = [carve(DIM) for _ in range(RX)]
        my = [carve(DIM) for _ in range(RY)]
        at[0] = loop_from
        sim = [carve(KS) for _ in range(2)]
        prob = carve(4 * KS).rearrange("p (h k) -> p h k", k=KS)
        th = carve(I)
        hs = carve(2 * I).rearrange("p (c q) -> p c q", q=SEQ)
        yT = carve(SEQ)
        xres = carve(TB * DIM).rearrange("p (t d) -> p t d", d=DIM)
        yg = carve(TB * TOPK * DIM).rearrange("p (t c d) -> p t c d", c=TOPK, d=DIM)
        z0, z1, z2 = (carve(TB * DIM).rearrange("p (t d) -> p t d", d=DIM) for _ in range(3))
        assert at[0] <= 11008
        probT = [sb(f"probT{i}", [P, 3 * P]) for i in range(2)]

        arena_r = sb("arena_r", [P, 3072], F32R)
        rt = [0]

        def carve_r(n):
            rt[0] += n
            return arena_r[:, rt[0] - n:rt[0]]

        xs1, xs2 = ([carve_r(SEQ), carve_r(SEQ)] for _ in range(2))
        mxT, mhT = ([[carve_r(n), carve_r(n)] for _ in range(r)] for n, r in ((P, RH), (I, 2)))
        rt[0] = 4 * SEQ
        oT = [[carve_r(SEQ), carve_r(SEQ)] for _ in range(2)]
        hss = [carve_r(2 * I), carve_r(2 * I)]
        opair = bank[4][:, 0:SEQ]
        pnT = sb("pnT", [96, SEQ], F32R)
        pnull = sb("pnull", [P, TB, HEADS * NNULL])
        nmx = sb("nmx", [P, HEADS, TB])
        den = sb("den", [P, HEADS, TB])
        rden = sb("rden", [P, HEADS, TB])
        ssq = [sb(f"ssq{i}", [P, HEADS // 2]) for i in range(2)]
        ssm, rpow, rnorm = (sb(n, [P, 8, HEADS // 2]) for n in ("ssm", "rpow", "rnorm"))
        xs_late = [sb(f"xs_late{i}", [P, SEQ], F32R) for i in range(2)]
        slot_now = sb("slot_now", [P, TB, TOPK], I32)
        w_now = sb("w_now", [P, TB, TOPK])

        rw_raw, rwT = sb("rw_raw", [E, DIM]), sb("rwT", [P, E])
        rbias = sb("rbias", [P, E])
        scratch = sq0.rearrange("p t d -> p (t d)")
        at[0] = 0

        def three_d(n, m):
            at[0] += n * m
            return scratch[:, at[0] - n * m:at[0]].rearrange("p (n m) -> p n m", m=m)

        lg, lth, pr, top, place = (three_d(NT, E) for _ in range(5))
        oh, pick = ([three_d(NT, E) for _ in range(TOPK)] for _ in range(2))
        tot, incl, excl, off = (three_d(E, NT) for _ in range(4))
        cmp = three_d(SLOT_TILES, E)
        topi = sb("topi", [P, NT, 8], U32)
        topf = sb("topf", [P, NT, TOPK])
        psum2, prec = sb("psum2", [P, NT]), sb("prec", [P, NT])
        iota_e, iota_s = sb("iota_e", [P, E]), sb("iota_s", [P, SLOT_TILES])
        ohs = sb("ohs", [P, NT, E], BF16)
        seg = sb("seg", [P, E, NT])
        ntile_i = sb("ntile_i", [P, E], I32)
        ntf, ntile, tend, tstart, base = (sb(n, [P, E]) for n in ("ntf", "ntile", "tend", "tstart", "base"))
        one8 = sb("one8", [P, E])
        slotf = sb("slotf", [P, NT, TOPK])
        tef, tef2 = sb("tef", [P, SLOT_TILES]), sb("tef2", [P, SLOT_TILES])

        xsum = [sb(f"xsum{i}", [P, NT]) for i in range(2)]
        nmean = [sb(f"nmean{i}", [P, NT]) for i in range(2)]
        vsum = [sb(f"vsum{i}", [P, NT]) for i in range(2)]
        var = [sb(f"var{i}", [P, NT]) for i in range(2)]
        rstd = [sb(f"rstd{i}", [P, NT]) for i in range(2)]

        qsc, ksc = sb("qsc", [P, 1]), sb("ksc", [P, 1])
        nraw = sb("nraw", [32, 2, DH])
        nsq, nss, nsm, nr = sb("nsq", [32, DH]), sb("nss", [32, 1]), sb("nsm", [32, 1]), sb("nr", [32, 1])
        nkT = sb("nkT", [P, HEADS * NNULL])
        nk2, nv2 = sb("nk2", [32, 2, DH]), sb("nv2", [32, 2, DH])
        nvT = probT[1][:, 0:PAIRS * 36]
        zeros = probT[0][:, 0:DIM]

        S = {n: sem(n) for n in [
            "x_in", "small_in", "gu_in", "d_in", "w_in", "o_in", "zero_in",
            "consts", "poolc", "xc1_ready", "sq_ready", "var_ready", "rstd_ready", "xn1_ready", "xn2_ready",
            "t_ps", "t_ev", "rw_ps", "rw_ev", "lg_ps", "lg_ready", "lth_ready", "ohs_ready", "rank_ps",
            "chain", "slots_ready", "scattered", "w_ps", "w_hi", "w_lo", "wraw_hi", "wraw_lo",
            "n_sm", "n_r", "n2_ready", "n_ps", "nvT_ready", "u_ps", "un_hi", "un_ready", "kdim_ready", "kt_zero", "kt_null",
            "nvz",
            "m_xps", "m_xhi", "m_xlo", "m_gups", "m_th", "m_ga", "m_h", "m_hps", "m_hhi", "m_hlo", "m_yps", "m_yev",
            "xhi", "xlo", "late_hi", "late_lo", "ksq", "red", "ssm_ready", "pw", "r_ready", "kqn",
            "sh_th", "sh_a", "sh_h", "sh_hi", "sh_lo", "shd",
            "sps", "ttr", "exp", "rd", "pn", "ptps", "ptev_a", "ptev_d", "pvd", "ohi", "olo", "oread",
            "pnc", "pn_hi", "pn_lo", "yev", "zc", "fin", "stored", "res_in", "gath", "passed", "now",
        ]}
        g = type("Sems", (), S)
        block = ctx.enter_context(nc.Block())
        m_in = [sem(f"m_in{r}") for r in range(RX)]
        filled = [sem(f"side{i}_filled") for i in range(2)]
        left = [sem(f"side{i}_left") for i in range(2)]
        m_out = [sem(f"m_out{r}") for r in range(RY)]

        def bc(ap, n):
            return ap.unsqueeze(2).to_broadcast([ap.shape[0], ap.shape[1], n])

        def front(ap, n):
            return ap.unsqueeze(1).to_broadcast([ap.shape[0], n, ap.shape[1]])

        def staged(first, drain, steps, lag):
            return {st: st - lag for st in steps if (not first or st >= lag) and (not drain or st < lag)}

        side = [bank[5], bank[7]]
        JOBS = [[(1, "next", "kq", 0, 1, 0), (2, "prev", "pn", 0, 0, 0), (4, "next", "kq", 0, 1, 1), (5, "next", "kq", 0, 0, 0),
                 (6, "next", "kq", 0, 0, 1), (7, "prev", "yt", 0, 0, 0), (8, "own", "v", 1, 0, 1), (11, "next", "kq", 1, 1, 1),
                 (12, "next", "kq", 1, 0, 0), (13, "next", "kq", 1, 0, 1), (14, "next", "v", 0, 0, 0), (15, "next", "v", 0, 0, 1)],
                [(0, "own", "tr", 1, 1, 0), (1, "own", "tr", 1, 1, 1), (2, "own", "tr", 1, 0, 0), (3, "own", "tr", 1, 0, 1),
                 (4, "own", "v", 1, 0, 0), (5, "own", "sh", 0, 0, 0), (7, "next", "kq", 1, 1, 0), (8, "own", "sh", 1, 0, 0),
                 (10, "next", "tr", 0, 1, 0), (11, "next", "tr", 0, 1, 1), (12, "next", "tr", 0, 0, 0), (13, "next", "tr", 0, 0, 1)]]
        FIRST_KQ = [[(0, "next", "kq", 0, 1, t), (1, "next", "kq", 0, 0, t), (2, "next", "kq", 1, 1, t), (3, "next", "kq", 1, 0, t)]
                    for t in range(TB)]
        READY = [[(0, "next", "tr", 0, 1, 0), (1, "next", "tr", 0, 0, 0), (2, "next", "v", 0, 0, 0)],
                 [(0, "next", "tr", 0, 1, 1), (1, "next", "tr", 0, 0, 1), (2, "next", "v", 0, 0, 1)]]
        PARTS = {"ahead": ("next",), "ready": ("next",), "first": ("next", "own"), "mid": ("next", "own", "prev"),
                 "last": ("own", "prev"), "drain": ("prev",)}

        def part_jobs(part, i):
            if part in ("ahead", "ready"):
                return (FIRST_KQ if part == "ahead" else READY)[i]
            return [job for job in JOBS[i] if job[1] in PARTS[part]]

        def count(part, i, until=HEADS):
            return sum(1 for job in part_jobs(part, i) if job[0] < until)

        def behind(part, b, s, lag):
            if s < lag:
                part, b, s = {"mid": "mid", "last": "mid", "drain": "last"}.get(part), b - 1, s + HEADS
            return [(part, b, job) for job in jobs(part, b, s - lag)] if part else []

        def jobs(part, b, s):
            found = []
            for i in range(2):
                for job in part_jobs(part, i):
                    if job[0] != s:
                        continue
                    n = count(part, i, s)
                    if part != "ahead":
                        n = n + count("ahead", i)
                        if part != "ready":
                            n = n + count("ready", i)
                            if part != "first":
                                n = n + count("first", i) - count("mid", i)
                                if part == "drain":
                                    n = n + count("last", i) - count("mid", i)
                                n = b * count("mid", i) + n
                    found.append((*job[2:], i, n))
            return found

        def nth(c, w, t):
            return 4 * c + 2 * (1 - w) + t

        def head_at(part, s, lag):
            h = s - lag
            return h if (("own" if h >= 0 else "prev") in PARTS[part]) else None

        groups = [([raw_gu[:, w, 2 * e + c, :] for w in range(2) for c in range(2)],
                   [t[:, e, :] for t in egu], "gu") for e in range(E)]
        groups += [([raw_d[:, e, c * P:(c + 1) * P] for e in (e2, e2 + 1) for c in range(2)],
                    [t[:, e2:e2 + 2, :].rearrange("p e n -> p (e n)") for t in ed], "d") for e2 in range(0, E, 2)]
        groups += [([raw_sgu[:, w, c, :] for w in range(2) for c in range(2)], [t[:] for t in sgu], "d"),
                   ([raw_sd[:, c * P:(c + 1) * P] for c in range(2)],
                    [t[:].rearrange("p c d -> p (c d)") for t in sd], "d")]
        EARLY = 4

        def settled(eng):
            eng.sem_inc(g.passed, 1)

        @block.sync
        def _(sync):
            xv = a["L0_attn_x"].rearrange("b (t p) d -> p (b t) d", p=P)
            sync.dma_start(x_all, xv).then_inc(g.x_in, 16)
            for w, n in enumerate(("L0_ffn_wg", "L0_ffn_wu")):
                sync.dma_start(raw_gu[:, w], a[n].rearrange("e (c p) h -> p (e c) h", p=P)).then_inc(g.gu_in, 16)
            sync.dma_start(raw_d, a["L0_ffn_wd"].rearrange("e p i -> p e i")).then_inc(g.d_in, 16)
            for w, n in enumerate(("L0_ffn_sg_w", "L0_ffn_su_w")):
                sync.dma_start(raw_sgu[:, w], a[n].rearrange("(c p) h -> p c h", p=P)).then_inc(g.d_in, 16)
            sync.dma_start(raw_sd, a["L0_ffn_sd_w"]).then_inc(g.d_in, 16)
            sync.dma_start(raw_w[:, 0:INNER], a["L0_attn_Wq"]).then_inc(g.w_in, 16)
            sync.dma_start(raw_w[:, INNER:3 * INNER], a["L0_attn_Wkv"]).then_inc(g.w_in, 16)
            sync.dma_start(raw_o, a["L0_attn_Wout"].rearrange("(c p) d -> p c d", p=P)).then_inc(g.o_in, 16)
            sync.wait_ge(g.nvz, 1)
            zv = xg_dram.rearrange("(p r) d -> p (r d)", p=P)
            for i in range(SLOT_TILES * DIM // 1280):
                sync.dma_start(zv[:, i * 1280:(i + 1) * 1280].rearrange("p (r w) -> p r w", w=DIM),
                               zeros.unsqueeze(1).to_broadcast([P, 10, DIM])).then_inc(g.zero_in, 16)

            sync.wait_ge(g.scattered, 16 * NT * TOPK)
            sync.wait_ge(g.wraw_lo, 3)

            def turn(it, first, drain, steps=range(MU)):
                load, store = (staged(first, drain, steps, lag) for lag in (0, 7))
                for st in steps:
                    if st in load:
                        j = load[st]
                        n = it * MU + j
                        if not first or j >= RX:
                            sync.wait_ge(g.m_xps, n - RX + 1)
                        sync.dma_start(mx_in[j % RX][:], xg_dram[bass.ds(n * P, P), :]).then_inc(m_in[j % RX], 16)
                    if st in store:
                        j = store[st]
                        n = it * MU + j
                        sync.wait_ge(g.m_yev, n + 1)
                        sync.dma_start(yg_dram[bass.ds(n * P, P), :], my[j % RY][:]).then_inc(m_out[j % RY], 16)

            turn(0, True, False)
            with sync.Fori(1, TURNS) as it:
                turn(it, False, False)
            turn(TURNS, False, True, range(7))

            ov = out.rearrange("b (t p) d -> b p t d", p=P)
            xb = a["L0_attn_x"].rearrange("b (t p) d -> b p t d", p=P)
            with sync.Fori(0, BATCH) as b:
                sync.wait_ge(g.fin, b + 1)
                sync.dma_start(xres, xb[bass.ds(b, 1)].rearrange("a p t d -> p (a t) d")).then_inc(g.res_in, 16)
                sync.wait_ge(g.fin, b + 2)
                sync.dma_start(ov[bass.ds(b, 1)].rearrange("a p t d -> p (a t) d"), z2).then_inc(g.stored, 16)
            sync.wait_ge(g.stored, 16 * (BATCH + 1))

        @block.gpsimd
        def _(pool):
            gp = nc.gpsimd
            gp.memset(zeros, 0.0).then_inc(g.nvz, 1)
            gp.memset(ident[:], 0.0).then_inc(g.poolc, 1)
            gp.memset(ones[:], 1.0).then_inc(g.poolc, 1)
            gp.memset(tri[:], 1.0).then_inc(g.poolc, 1)
            gp.memset(mhalf[:], -0.5).then_inc(g.poolc, 1)
            gp.memset(seg[:], 1.0).then_inc(g.poolc, 1)
            gp.memset(one8[:], 1.0).then_inc(g.poolc, 1)
            gp.memset(nvT, 0.0).then_inc(g.poolc, 1)
            for h in range(HEADS):
                gp.memset(rslope[:, h:h + 1], 1.0 / SLOPES[h]).then_inc(g.poolc, 1)
            gp.iota(iota_e[:], [[1, E]], base=0, channel_multiplier=0, allow_small_or_imprecise_dtypes=True).then_inc(g.poolc, 1)
            gp.iota(iota_s[:], [[1, SLOT_TILES]], base=0, channel_multiplier=0, allow_small_or_imprecise_dtypes=True).then_inc(g.poolc, 1)
            gp.iota(bias[:, 0:K0], [[1, K0]], base=-NNULL, channel_multiplier=-1, allow_small_or_imprecise_dtypes=True).then_inc(g.poolc, 1)
            gp.iota(bias[:, K0:KS], [[1, K1]], base=-NNULL - P, channel_multiplier=-1, allow_small_or_imprecise_dtypes=True).then_inc(g.poolc, 1)
            pool.wait_ge(g.poolc, 27)
            gp.affine_select(out=ident[:], in_=ident[:], compare_op=ALU.not_equal, fill=1.0, base=0,
                             pattern=[[-1, P]], channel_multiplier=1).then_inc(g.consts, 1)
            gp.affine_select(out=tri[:], in_=tri[:], compare_op=ALU.is_gt, fill=0.0, base=0,
                             pattern=[[1, P]], channel_multiplier=-1).then_inc(g.consts, 1)
            gp.memset(seg[:, :, 0:1], 0.0).then_inc(g.consts, 1)
            gp.affine_select(out=bias[:, 0:K0], in_=bias[:, 0:K0], compare_op=ALU.is_ge, fill=MASKED, base=NNULL,
                             pattern=[[-1, K0]], channel_multiplier=1).then_inc(g.consts, 1)
            gp.affine_select(out=bias[:, K0:KS], in_=bias[:, K0:KS], compare_op=ALU.is_ge, fill=MASKED, base=NNULL + P,
                             pattern=[[-1, K1]], channel_multiplier=1).then_inc(g.consts, 1)
            for i in range(2):
                pool.wait_ge(g.var_ready, i + 1)
                gp.tensor_tensor(rstd[i][:], var[i][:], mhalf[:, 0:NT], ALU.pow).then_inc(g.rstd_ready, 1)
            pool.wait_ge(g.n_sm, 1)
            gp.tensor_tensor(nr[:], nsm[:], mhalf[0:32, 0:1], ALU.pow).then_inc(g.n_r, 1)
            pool.wait_ge(g.t_ev, 8)
            gp.memset(arena_a[:, 0:HEADS * K1], 0.0).then_inc(g.kt_zero, 1)
            pool.wait_ge(g.slots_ready, 1)
            pool.wait_ge(g.zero_in, 16 * (SLOT_TILES * DIM // 1280))

            def scatter(n):
                pool.indirect_dma_start(xg_dram, bass.IndirectOffsetOnAxis(ap=slot[:, n // TOPK, n % TOPK:n % TOPK + 1], axis=0),
                                        xn1[:, n // TOPK, :], None).then_inc(g.scattered, 16)

            def norms(b, job):
                kind, c, w, t, i, n = job
                if kind == "kq":
                    j = nth(c, w, t)
                    nb = b + 1
                    pool.wait_ge(g.ssm_ready, 8 * nb + j + 1)
                    if w == 0:
                        gp.tensor_tensor(rnorm[:, j, :], ssm[:, j, :], mhalf[:, 0:HEADS // 2],
                                         ALU.pow).then_inc(g.r_ready, 1)
                    else:
                        gp.tensor_tensor(rpow[:, j, :], ssm[:, j, :], mhalf[:, 0:HEADS // 2],
                                         ALU.pow).then_inc(g.pw, 1)
                        pool.wait_ge(g.pw, 4 * nb + 2 * c + t + 1)
                        gp.tensor_tensor(rnorm[:, j, :], rpow[:, j, :], rslope[:, c * 8:c * 8 + 8],
                                         ALU.mult).then_inc(g.r_ready, 1)

            def scale_by_norm(b, job):
                kind, c, w, t, i, n = job
                if kind == "kq":
                    j = nth(c, w, t)
                    pool.wait_ge(g.r_ready, 8 * (b + 1) + j + 1)
                    pool.wait_ge(left[i], n + 1)
                    rows = (qtok if w else ktok)[t][:, c * 512:(c + 1) * 512].rearrange("p (h d) -> p h d", d=DH)
                    gp.tensor_tensor(rows, rows, bc(rnorm[:, j, :], DH), ALU.mult).then_inc(g.kqn, 1)

            def entry(part, b, steps=range(HEADS)):
                whose = PARTS[part]
                nb = b + 1
                for s in steps:
                    if s < 2 and "next" in whose and part != "ready":
                        xT, xs = ((xn2T, xs2), (xn1T, xs1))[s]
                        for _, _, (kind, c, w, t, i, n) in (x for lag in range(1, HEADS) for x in behind(part, b, s, lag)):
                            if (kind, c, w, t) == (("kq", 1, 1, 1), ("v", 0, 0, 1))[s]:
                                pool.wait_ge(filled[i], n + 1)
                        if part == "first":
                            for i in range(2):
                                pool.wait_ge(filled[i], count("ahead", i) + count("ready", i))
                        settled(pool)
                        gp.tensor_copy(xs[0], xT[:, bass.ds(nb * SEQ, SEQ)]).then_inc(g.xhi, 1)
                        pool.wait_ge(g.xhi, 2 * nb + s + 1)
                        settled(pool)
                        gp.tensor_tensor(xs[1], xT[:, bass.ds(nb * SEQ, SEQ)], xs[0].bitcast(F32),
                                         ALU.subtract).then_inc(g.xlo, 1)
                    if s in (7, 10) and "own" in whose:
                        c = (7, 10).index(s)
                        pool.wait_ge(g.sh_h, 2 * b + c + 1)
                        if part != "first":
                            pool.wait_ge(g.shd, b)
                        settled(pool)
                        gp.tensor_copy(hss[0][:, c * SEQ:(c + 1) * SEQ], hs[:, c, :]).then_inc(g.sh_hi, 1)
                        pool.wait_ge(g.sh_hi, 2 * b + c + 1)
                        gp.tensor_tensor(hss[1][:, c * SEQ:(c + 1) * SEQ], hs[:, c, :],
                                         hss[0][:, c * SEQ:(c + 1) * SEQ].bitcast(F32), ALU.subtract).then_inc(g.sh_lo, 1)
                    if s == 2 and "own" in whose:
                        for _, _, (kind, c, _, t, i, n) in (x for lag in range(1, HEADS) for x in behind(part, b, s, lag)):
                            if (kind, c) == ("sh", 1):
                                pool.wait_ge(filled[i], n + 1)
                        settled(pool)
                        gp.tensor_copy(xs_late[0][:], xn1T[:, bass.ds(b * SEQ, SEQ)]).then_inc(g.late_hi, 1)
                        pool.wait_ge(g.late_hi, b + 1)
                        settled(pool)
                        gp.tensor_tensor(xs_late[1][:], xn1T[:, bass.ds(b * SEQ, SEQ)], xs_late[0][:].bitcast(F32),
                                         ALU.subtract).then_inc(g.late_lo, 1)
                    h = head_at(part, s, 2)
                    for _, job_b, job in (behind(part, b, s, 1) if part != "ahead" else []):
                        norms(job_b, job)
                        scale_by_norm(job_b, job)
                    if h is not None and h % 2:
                        p = h // 2
                        pool.wait_ge(g.pn, TB * (HEADS * b + h + 1))
                        if p == 0 and part != "first":
                            pool.wait_ge(g.pn_hi, 2 * b)
                        settled(pool)
                        q = p % PAIRS
                        two = prob[:, h % 4 - 1:h % 4 + 1, :]
                        for t, c0 in ((0, 0), (1, K0)):
                            gp.tensor_copy(pnull[:, t, 4 * q:4 * q + 4].rearrange("p (h n) -> p h n", n=2),
                                           two[:, :, c0:c0 + NNULL]).then_inc(g.pnc, 1)
                    if s == 10 and "own" in whose:
                        pool.wait_ge(g.fin, b + 1)
                        settled(pool)
                        gp.tensor_copy(slot_now[:], slot[:, bass.ds(b * TB, TB), :]).then_inc(g.now, 1)
                        gp.tensor_copy(w_now[:], wts[:, bass.ds(b * TB, TB), :]).then_inc(g.now, 1)
                        pool.wait_ge(g.now, 2 * b + 2)
                        settled(pool)
                        for t in range(TB):
                            for c in range(TOPK):
                                pool.indirect_dma_start(yg[:, t, c, :], None, yg_dram,
                                                        bass.IndirectOffsetOnAxis(ap=slot_now[:, t, c:c + 1], axis=0)
                                                        ).then_inc(g.gath, 16)

            for n in range(NT * TOPK):
                if n in (15, 22):
                    entry("ahead", -1, [n // 22])
                scatter(n)
            for s in range(AHEAD):
                for _, job_b, job in behind("ahead", -1, s, 1):
                    norms(job_b, job)
                    scale_by_norm(job_b, job)
            for r in range(RY):
                pool.wait_ge(m_out[r], 16 * (SLOT_TILES // RY))
            entry("first", 0)
            with pool.Fori(1, BATCH - 1) as b:
                entry("mid", b)
            entry("last", BATCH - 1)
            entry("drain", BATCH, range(DRAIN))

        @block.scalar
        def _(act):
            sc = nc.scalar
            col = [("L0_attn_norm_g", g_col[:]), ("L0_attn_norm_b", b_col[:])]
            col += [(f"L0_attn_{w}_scale", t[r:r + DH, :]) for w, t in (("q", qsc), ("k", ksc)) for r in (0, DH)]
            for n, t in col:
                act.dma_start(t, a[n].rearrange("(p o) -> p o", o=1)).then_inc(g.small_in, 16)
            act.dma_start(nraw[:], a["L0_attn_null_kv"].rearrange("h (n w) d -> (h n) w d", w=2)).then_inc(g.small_in, 16)
            act.dma_start(rw_raw[:], a["L0_ffn_router_w"]).then_inc(g.small_in, 16)
            act.dma_start(rbias[:], a["L0_ffn_routing_bias"].rearrange("(o e) -> o e", o=1).to_broadcast([P, E])).then_inc(g.small_in, 16)

            def split_group(n):
                srcs, dst, _ = groups[n]
                w = len(srcs) * P
                act.wait_ge(g.w_ps, n + 1)
                sc.activation(dst[0], bank[n % EARLY][:, 0:w], ACT.Copy).then_inc(g.w_hi, 1)

            act.wait_ge(g.xc1_ready, 1)
            sc.activation(sq0, xc, ACT.Square).then_inc(g.sq_ready, 1)
            for n in range(EARLY):
                split_group(n)
            act.wait_ge(g.rw_ps, 1)
            sc.activation(rwT[:], bank[7][:, 0:E], ACT.Copy).then_inc(g.rw_ev, 1)
            for i in range(4):
                act.wait_ge(g.t_ps, i + 1)
                sc.activation(xn1T[:, i * 512:(i + 1) * 512], bank[4 + i % 2][:], ACT.Copy).then_inc(g.t_ev, 1)
            act.wait_ge(g.xc1_ready, 2)
            sc.activation(sq0, xc, ACT.Square).then_inc(g.sq_ready, 1)
            act.wait_ge(g.w_in, 32)
            sc.activation(wq[0][:], raw_w[:, 0:INNER], ACT.Copy).then_inc(g.wraw_hi, 1)
            act.wait_ge(g.lg_ready, 1)
            sc.activation(lth, lg, ACT.Tanh, scale=0.5).then_inc(g.lth_ready, 1)
            act.wait_ge(g.o_in, 16)
            sc.activation(wkv[0][:], raw_w[:, INNER:3 * INNER], ACT.Copy).then_inc(g.wraw_hi, 1)
            sc.activation(wo[0][:], raw_o, ACT.Copy).then_inc(g.wraw_hi, 1)
            act.wait_ge(g.small_in, 16 * 9)
            for i in range(4):
                act.wait_ge(g.t_ps, 4 + i + 1)
                sc.activation(xn2T[:, i * 512:(i + 1) * 512], bank[4 + i % 2][:], ACT.Identity,
                              scale=g_col[:, 0:1], bias=b_col[:, 0:1]).then_inc(g.t_ev, 1)
            act.wait_ge(g.n_ps, 2)
            act.wait_ge(g.kdim_ready, 1)
            sc.activation(nkT[:], bank[7][:, 64:96], ACT.Copy, scale=kdim[:, 0:1]).then_inc(g.nvT_ready, 1)
            for r, base_p in ((0, 0), (2, DH)):
                sc.activation(nvT[base_p:base_p + DH, :].rearrange("p (q c) -> p q c", c=36)[:, :, r:r + 2],
                              bank[7][base_p:base_p + DH, 96:128].rearrange("p (q c) -> p q c", c=4)[:, :, r:r + 2],
                              ACT.Copy).then_inc(g.nvT_ready, 1)
            act.wait_ge(g.u_ps, 1)
            for r in (0, 32):
                sc.activation(unull[r:r + 32, :], bank[7][0:32, 256:256 + DIM], ACT.Copy).then_inc(g.un_hi, 1)
            for n in range(EARLY, len(groups)):
                split_group(n)

            act.wait_ge(g.kt_zero, 1)
            for half in range(2):
                r = slice(half * DH, half * DH + DH)
                sc.activation(kT[r, half:HEADS:2, 0:NNULL],
                              nkT[r, :].rearrange("p (q c) -> p q c", c=4)[:, :, 2 * half:2 * half + 2],
                              ACT.Copy).then_inc(g.kt_null, 1)
            def side_out(part, b, job):
                kind, c, w, t, i, n = job
                nb = b + 1
                if kind != "yt":
                    act.wait_ge(filled[i], n + 1)
                if kind == "kq":
                    j = nth(c, w, t)
                    if part != "ahead" or j >= 2:
                        act.wait_ge(g.ssm_ready, 8 * nb + j - 1)
                    sc.activation(sqb[j % 2], side[i][:], ACT.Square).then_inc(g.ksq, 1)
                    sc.activation((qtok if w else ktok)[t][:, c * 512:(c + 1) * 512], side[i][:], ACT.Copy).then_inc(left[i], 1)
                if kind == "tr":
                    if c == 0 and part != "ready":
                        act.wait_ge(g.sps, HEADS * b + HEADS // 2)
                    if c == 1 and part != "first":
                        act.wait_ge(g.sps, HEADS * b)
                    tt = slice(t * P, (t + 1) * P)
                    if w == 0:
                        for half in range(2):
                            r = slice(half * DH, half * DH + DH)
                            ins = sc.activation(kT[r, 8 * c + half:8 * c + 8:2, NNULL + t * P:NNULL + (t + 1) * P],
                                                side[i][r, :].rearrange("p (q k) -> p q k", k=P), ACT.Copy,
                                                scale=kdim[r, 0:1])
                    else:
                        ins = sc.activation(qT[:, 4 * c:4 * c + 4, tt],
                                            side[i][:].rearrange("p (q k) -> p q k", k=P), ACT.Copy)
                    ins.then_inc(left[i], 1)
                if kind == "v":
                    if part == "ready":
                        act.wait_ge(g.scattered, 16 * NT * TOPK)
                    if c == 0 and part != "ready":
                        act.wait_ge(g.pvd, PAIRS * b + PAIRS // 2)
                    if c == 1 and part != "first":
                        act.wait_ge(g.pvd, PAIRS * b)
                    sc.activation(v[:, t, c * 512:(c + 1) * 512], side[i][:], ACT.Copy).then_inc(left[i], 1)
                if kind == "sh":
                    if part != "first" or c:
                        act.wait_ge(g.sh_h, 2 * b + c)
                    sc.activation(th, side[i][:, 0:SEQ], ACT.Tanh, scale=0.5).then_inc(g.sh_th, 1)
                if kind == "pn":
                    for r in (0, 64):
                        sc.activation(pnT[r:r + 32, :], side[i][0:32, 0:SEQ], ACT.Copy).then_inc(g.pn_hi, 1)

            def entry(part, b, steps=range(HEADS)):
                whose = PARTS[part]
                nb = b + 1
                for s in steps:
                    h = head_at(part, s, 5)
                    if h is not None and h % 2:
                        p = h // 2
                        act.wait_ge(g.pvd, PAIRS * b + p + 1)
                        if part != "first" or p >= 2:
                            act.wait_ge(g.oread, PAIRS * b + p - 1)
                        sc.activation(oT[p % 2][0], opair, ACT.Copy).then_inc(g.ohi, 1)
                    for job in behind(part, b, s, 1):
                        side_out(*job)
                    h = head_at(part, s, 3)
                    if h is not None and h % 2 == 1:
                        act.wait_ge(g.ptps, HEADS * b + h + 1)
                        if part != "first" or h >= 2:
                            act.wait_ge(g.pvd, PAIRS * b + h // 2)
                        sc.activation(probT[1][:], bank[3][:, 0:3 * P], ACT.Copy).then_inc(g.ptev_a, 1)
                    if s == 6 and "prev" in whose:
                        act.wait_ge(g.oread, PAIRS * b)
                        act.wait_ge(g.fin, b)
                        sc.activation(yT, bank[6][:, 0:SEQ], ACT.Copy).then_inc(g.yev, 1)
                    h = head_at(part, s, 1)
                    if h is not None:
                        if part != "first" or h >= 4:
                            act.wait_ge(g.ptps, HEADS * b + h - 3)
                            act.wait_ge(g.pnc, 2 * (PAIRS * b + h // 2 - 1))
                        act.wait_ge(g.ttr, TB * (HEADS * b + h + 1))
                        for t, c in ((0, slice(0, K0)), (1, slice(K0, KS))):
                            sc.activation(prob[:, h % 4, c], sim[h % 2][:, c], ACT.Exp, scale=-1.0,
                                          bias=nmx[:, h % HEADS, t:t + 1],
                                          accum_out=den[:, h % HEADS, t:t + 1]).then_inc(g.exp, 1)

            entry("ahead", -1, range(AHEAD))

            def turn(it, first, drain, steps=range(MU)):
                ys, xs, hs, tanh = (staged(first, drain, steps, lag) for lag in (6, 0, 4, 2))
                for st in steps:
                    if st in ys:
                        j = ys[st]
                        n = it * MU + j
                        act.wait_ge(g.m_yps, n + 1)
                        if not first or j >= RY:
                            act.wait_ge(m_out[j % RY], 16 * (it * (MU // RY) + j // RY))
                        sc.activation(my[j % RY], bank[6 + j % 2][:, 0:DIM], ACT.Copy).then_inc(g.m_yev, 1)
                    if st in xs:
                        j = xs[st]
                        n = it * MU + j
                        act.wait_ge(g.m_xps, n + 1)
                        if not first or j >= RH:
                            act.wait_ge(g.m_gups, n - RH + 1)
                        sc.activation(mxT[j % RH][0], bank[j % 2][:, 0:P], ACT.Copy).then_inc(g.m_xhi, 1)
                    if st in hs:
                        j = hs[st]
                        n = it * MU + j
                        act.wait_ge(g.m_hps, n + 1)
                        if not first or j >= 2:
                            act.wait_ge(g.m_yps, n - 1)
                        sc.activation(mhT[j % 2][0], bank[4 + j % 2][:, 0:I], ACT.Copy).then_inc(g.m_hhi, 1)
                    if st in tanh:
                        j = tanh[st]
                        n = it * MU + j
                        act.wait_ge(g.m_gups, n + 1)
                        if not first or j >= 2:
                            act.wait_ge(g.m_ga, n - 1)
                        sc.activation(mth[j % 2], bank[2 + j % 2][:, 0:I], ACT.Tanh, scale=0.5).then_inc(g.m_th, 1)

            turn(0, True, False)
            with act.Fori(1, TURNS) as it:
                turn(it, False, False)
            turn(TURNS, False, True, range(6))

            entry("ready", -1, range(4))
            for r in range(RY):
                act.wait_ge(m_out[r], 16 * (SLOT_TILES // RY))
            entry("first", 0)
            with act.Fori(1, BATCH - 1) as b:
                entry("mid", b)
            entry("last", BATCH - 1)
            entry("drain", BATCH, range(DRAIN))

        @block.vector
        def _(dve):
            ve = nc.vector
            chain = [0]

            def link(ins):
                chain[0] += 1
                ins.then_inc(g.chain, 1)
                dve.wait_ge(g.chain, chain[0])

            def split_group(n):
                srcs, dst, _ = groups[n]
                w = len(srcs) * P
                dve.wait_ge(g.w_hi, n + 1)
                ve.tensor_tensor(dst[1], bank[n % EARLY][:, 0:w], dst[0].bitcast(F32), ALU.subtract).then_inc(g.w_lo, 1)

            dve.wait_ge(g.x_in, 16)
            for i, (src, dst) in enumerate(((x_all, xn1), (xn1, x_all))):
                link(ve.reduce_sum(xsum[i][:], src, AX.X))
                link(ve.tensor_scalar(nmean[i][:], xsum[i][:], -1.0 / DIM, None, ALU.mult))
                ve.tensor_tensor(xc, src, bc(nmean[i][:], DIM), ALU.add).then_inc(g.xc1_ready, 1)
                dve.wait_ge(g.sq_ready, i + 1)
                link(ve.reduce_sum(vsum[i][:], sq0, AX.X))
                ve.tensor_scalar(var[i][:], vsum[i][:], 1.0 / DIM, LN_EPS, ALU.mult, ALU.add).then_inc(g.var_ready, 1)
                if i == 0:
                    for n in range(EARLY):
                        split_group(n)
                if i == 0:
                    dve.wait_ge(g.rstd_ready, 1)
                    dve.wait_ge(g.xc1_ready, 1)
                    ve.tensor_tensor(dst, xc, bc(rstd[i][:], DIM), ALU.mult).then_inc(g.xn1_ready, 1)
                    dve.wait_ge(g.xn1_ready, 1)
            dve.wait_ge(g.small_in, 16 * 9)
            dve.wait_ge(g.lg_ps, 1)
            ve.tensor_tensor(lg, bank[6][:, 0:NT * E].rearrange("p (t e) -> p t e", e=E), front(rbias[:], NT),
                             ALU.add).then_inc(g.lg_ready, 1)
            dve.wait_ge(g.rstd_ready, 2)
            dve.wait_ge(g.xc1_ready, 2)
            ve.tensor_tensor(x_all, xc, bc(rstd[1][:], DIM), ALU.mult).then_inc(g.xn2_ready, 1)
            link(ve.tensor_tensor(nsq[:], nraw[:, 0, :], nraw[:, 0, :], ALU.mult))
            link(ve.reduce_sum(nss[:], nsq[:], AX.X))
            ve.tensor_scalar(nsm[:], nss[:], L2_EPS2, None, ALU.max).then_inc(g.n_sm, 1)
            link(ve.tensor_scalar(kdim[:], qsc[:], SIM_SCALE, None, ALU.mult))
            ve.tensor_tensor(kdim[:], kdim[:], ksc[:], ALU.mult).then_inc(g.kdim_ready, 1)
            ve.tensor_copy(nv2[:, 0, :], nraw[:, 1, :]).then_inc(g.n2_ready, 1)
            ve.tensor_copy(nv2[:, 1, :], nraw[:, 1, :]).then_inc(g.n2_ready, 1)
            dve.wait_ge(g.lth_ready, 1)
            link(ve.tensor_scalar(pr, lth, 0.5, 0.5, ALU.mult, ALU.add))
            for k in range(NT):
                last = ve.max(top[:, k, :], pr[:, k, :])
            link(last)
            for k in range(NT):
                last = ve.max_index(topi[:, k, :], top[:, k, :], pr[:, k, :])
            link(last)
            link(ve.tensor_copy(topf[:], topi[:, :, 0:TOPK]))
            ve.tensor_tensor(psum2[:], top[:, :, 0], top[:, :, 1], ALU.add)
            dve.wait_ge(g.consts, 3)
            for c in range(TOPK):
                last = ve.tensor_tensor(oh[c], front(iota_e[:], NT), bc(topf[:, :, c], E), ALU.is_equal)
            link(last)
            ve.tensor_tensor(ohs[:], oh[0], oh[1], ALU.add).then_inc(g.ohs_ready, 1)
            link(ve.reciprocal(prec[:], psum2[:]))
            link(ve.tensor_tensor(wts[:], top[:, :, 0:TOPK], bc(prec[:], TOPK), ALU.mult))
            dve.wait_ge(g.rank_ps, 1)
            link(ve.tensor_copy(tot, bank[6][:, P:2 * P].rearrange("p (t e) -> p e t", e=E)))
            link(ve.tensor_tensor_scan(incl.rearrange("p e t -> p (e t)"), seg[:].rearrange("p e t -> p (e t)"),
                                       tot.rearrange("p e t -> p (e t)"), 0.0, ALU.mult, ALU.add))
            link(ve.tensor_scalar(ntf[:], incl[:, :, NT - 1], 1.0 / P, (P - 1.0) / (2 * P), ALU.mult, ALU.add))
            link(ve.tensor_copy(ntile_i[:], ntf[:]))
            link(ve.tensor_copy(ntile[:], ntile_i[:]))
            link(ve.tensor_tensor_scan(tend[:], one8[:], ntile[:], 0.0, ALU.mult, ALU.add))
            link(ve.tensor_tensor(tstart[:], tend[:], ntile[:], ALU.subtract))
            link(ve.tensor_scalar(base[:], tstart[:], float(P), None, ALU.mult))
            link(ve.tensor_tensor(excl, incl, tot, ALU.subtract))
            link(ve.tensor_tensor(off, excl, bc(base[:], NT), ALU.add))
            link(ve.tensor_tensor(place, bank[6][:, 0:P].rearrange("p (t e) -> p t e", e=E),
                                  off.rearrange("p e t -> p t e"), ALU.add))
            for c in range(TOPK):
                link(ve.tensor_tensor(pick[c], oh[c], place, ALU.mult))
                link(ve.reduce_sum(slotf[:, :, c], pick[c], AX.X))
            ve.tensor_copy(slot[:], slotf[:]).then_inc(g.slots_ready, 1)
            link(ve.tensor_tensor(cmp, bc(iota_s[:], E), front(tstart[:], SLOT_TILES), ALU.is_ge))
            link(ve.reduce_sum(tef[:], cmp, AX.X))
            link(ve.tensor_scalar(tef2[:], tef[:], -1.0, None, ALU.add))
            ve.tensor_copy(tile_expert[:], tef2[:]).then_inc(g.slots_ready, 1)
            dve.wait_ge(g.n_r, 1)
            for i in range(2):
                ve.tensor_scalar(nk2[:, i, :], nraw[:, 0, :], nr[:, 0:1], None, ALU.mult).then_inc(g.n2_ready, 1)
            dve.wait_ge(g.un_hi, 2)
            ve.tensor_tensor(unull[64:96, :], bank[7][0:32, 256:256 + DIM], unull[0:32, :].bitcast(F32),
                             ALU.subtract).then_inc(g.un_ready, 1)
            for n in range(EARLY, len(groups)):
                split_group(n)
            dve.wait_ge(g.wraw_hi, 3)
            ve.tensor_tensor(wq[1][:], raw_w[:, 0:INNER], wq[0][:].bitcast(F32), ALU.subtract).then_inc(g.wraw_lo, 1)
            ve.tensor_tensor(wkv[1][:], raw_w[:, INNER:3 * INNER], wkv[0][:].bitcast(F32), ALU.subtract).then_inc(g.wraw_lo, 1)
            ve.tensor_tensor(wo[1][:], raw_o, wo[0][:].bitcast(F32), ALU.subtract).then_inc(g.wraw_lo, 1)

            dve.sem_inc(g.fin, 1)
            dve.sem_inc(g.stored, 16)
            def side_out(part, b, job):
                kind, c, w, t, i, n = job
                nb = b + 1
                if kind == "sh":
                    dve.wait_ge(g.sh_th, 2 * b + c + 1)
                    ve.scalar_tensor_tensor(out=th, in0=th, scalar=1.0, in1=side[i][:, 0:SEQ],
                                            op0=ALU.add, op1=ALU.mult).then_inc(g.sh_a, 1)
                    dve.wait_ge(g.sh_a, 2 * b + c + 1)
                    ve.scalar_tensor_tensor(out=hs[:, c, :], in0=th, scalar=0.5, in1=side[i][:, SEQ:2 * SEQ],
                                            op0=ALU.mult, op1=ALU.mult).then_inc(g.sh_h, 1)
                    dve.wait_ge(g.sh_h, 2 * b + c + 1)
                    dve.sem_inc(left[i], 1)
                if kind == "pn":
                    dve.wait_ge(g.pn_hi, 2 * b)
                    ve.tensor_tensor(pnT[32:64, :], side[i][0:32, 0:SEQ], pnT[0:32, :].bitcast(F32),
                                     ALU.subtract).then_inc(g.pn_lo, 1)
                    dve.wait_ge(g.pn_lo, b)
                    dve.sem_inc(left[i], 1)
                if kind == "yt":
                    dve.wait_ge(filled[i], n + 1)
                    dve.wait_ge(g.res_in, 16 * b)
                    dve.wait_ge(g.gath, 16 * TB * TOPK * b)
                    dve.wait_ge(g.stored, 16 * b)
                    ve.tensor_tensor(z0, side[i][:, 0:SEQ].rearrange("p (t d) -> p t d", d=DIM), xres,
                                     ALU.add).then_inc(g.zc, 1)
                    for k, (src, dst) in enumerate(((z0, z1), (z1, z2))):
                        dve.wait_ge(g.zc, 2 * b - 1 + k)
                        if k == 0:
                            dve.sem_inc(left[i], 1)
                        for tt in range(TB):
                            ins = ve.scalar_tensor_tensor(out=dst[:, tt, :], in0=yg[:, tt, k, :],
                                                          scalar=w_now[:, tt, k:k + 1], in1=src[:, tt, :],
                                                          op0=ALU.mult, op1=ALU.add)
                        ins.then_inc(g.zc if k == 0 else g.fin, 1)
                if kind == "kq":
                    j = nth(c, w, t)
                    dve.wait_ge(g.ksq, 8 * nb + j + 1)
                    ve.reduce_sum(ssq[j % 2][:], sqb[j % 2].rearrange("p (h d) -> p h d", d=DH), AX.X).then_inc(g.red, 1)
                    dve.wait_ge(g.red, 8 * nb + j + 1)
                    if part != "ahead":
                        dve.wait_ge(g.r_ready, 8 * nb + j - 7)
                    ve.tensor_scalar(ssm[:, j, :], ssq[j % 2][:], L2_EPS2, None, ALU.max).then_inc(g.ssm_ready, 1)

            def entry(part, b, steps=range(HEADS)):
                whose = PARTS[part]
                nb = b + 1
                for s in steps:
                    h = head_at(part, s, 5)
                    if h is not None and h % 2:
                        p = h // 2
                        dve.wait_ge(g.ohi, PAIRS * b + p + 1)
                        ve.tensor_tensor(oT[p % 2][1], opair, oT[p % 2][0].bitcast(F32),
                                         ALU.subtract).then_inc(g.olo, 1)
                    h = head_at(part, s, 2)
                    if h is not None:
                        dve.wait_ge(g.exp, TB * (HEADS * b + h + 1))
                        ve.reciprocal(rden[:, h % HEADS, :], den[:, h % HEADS, :]).then_inc(g.rd, 1)
                        dve.wait_ge(g.rd, HEADS * b + h + 1)
                        for t, c in ((0, slice(0, K0)), (1, slice(K0, KS))):
                            pr = prob[:, h % 4, c]
                            ve.tensor_scalar(pr, pr, rden[:, h % HEADS, t:t + 1], None, ALU.mult).then_inc(g.pn, 1)
                    h = head_at(part, s, 3)
                    for job in behind(part, b, s, 1):
                        side_out(*job)
                    if h is not None and h % 2 == 0:
                        dve.wait_ge(g.ptps, HEADS * b + h + 1)
                        if part != "first" or h >= 2:
                            dve.wait_ge(g.pvd, PAIRS * b + h // 2)
                        ve.tensor_copy(probT[0][:], bank[2][:, 0:3 * P]).then_inc(g.ptev_d, 1)
                    h = head_at(part, s, 0)
                    if h is not None:
                        dve.wait_ge(g.sps, HEADS * b + h + 1)
                        if part != "first" or h >= 2:
                            dve.wait_ge(g.exp, TB * (HEADS * b + h - 1))
                        settled(dve)
                        for t, c in ((0, slice(0, K0)), (1, slice(K0, KS))):
                            ve.tensor_tensor_reduce(out=sim[h % 2][:, c], in0=bank[h % 2][:, c], in1=bias[:, c],
                                                    scale=-SLOPES[h], scalar=3e38, op0=ALU.add, op1=ALU.min,
                                                    accum_out=nmx[:, h, t:t + 1]).then_inc(g.ttr, 1)

            entry("ahead", -1, range(AHEAD))

            def turn(it, first, drain, steps=range(MU)):
                xs, hs, mid = (staged(first, drain, steps, lag) for lag in (0, 4, 2))
                for st in steps:
                    if st in xs:
                        j = xs[st]
                        n = it * MU + j
                        dve.wait_ge(g.m_xhi, n + 1)
                        if not first or j >= RH:
                            dve.wait_ge(g.m_gups, n - RH + 1)
                        ve.tensor_tensor(mxT[j % RH][1], bank[j % 2][:, 0:P], mxT[j % RH][0].bitcast(F32),
                                         ALU.subtract).then_inc(g.m_xlo, 1)
                    if st in hs:
                        j = hs[st]
                        n = it * MU + j
                        dve.wait_ge(g.m_hhi, n + 1)
                        ve.tensor_tensor(mhT[j % 2][1], bank[4 + j % 2][:, 0:I], mhT[j % 2][0].bitcast(F32),
                                         ALU.subtract).then_inc(g.m_hlo, 1)
                    if st in mid:
                        j = mid[st]
                        n = it * MU + j
                        ps = bank[2 + j % 2]
                        dve.wait_ge(g.m_th, n + 1)
                        ve.scalar_tensor_tensor(out=mga[j % 2], in0=mth[j % 2], scalar=1.0, in1=ps[:, 0:I],
                                                op0=ALU.add, op1=ALU.mult).then_inc(g.m_ga, 1)
                        dve.wait_ge(g.m_ga, n + 1)
                        if not first or j >= RH:
                            dve.wait_ge(g.m_hps, n - RH + 1)
                        ve.scalar_tensor_tensor(out=mh[j % RH], in0=mga[j % 2], scalar=0.5, in1=ps[:, I:2 * I],
                                                op0=ALU.mult, op1=ALU.mult).then_inc(g.m_h, 1)

            turn(0, True, False)
            with dve.Fori(1, TURNS) as it:
                turn(it, False, False)
            turn(TURNS, False, True, range(4))

            for r in range(RY):
                dve.wait_ge(m_out[r], 16 * (SLOT_TILES // RY))
            entry("first", 0)
            with dve.Fori(1, BATCH - 1) as b:
                entry("mid", b)
            entry("last", BATCH - 1)
            entry("drain", BATCH, range(DRAIN))

        @block.tensor
        def _(pe):
            te = nc.tensor

            def three(dst, lhs, rhs, first, last):
                te.matmul(dst, lhs[0], rhs[0], start=first, stop=False)
                te.matmul(dst, lhs[1], rhs[0], start=False, stop=False)
                return te.matmul(dst, lhs[0], rhs[1], start=False, stop=last)

            def transpose_group(n):
                srcs, _, _ = groups[n]
                if n == 0:
                    pe.wait_ge(g.gu_in, 32)
                if n == E:
                    pe.wait_ge(g.d_in, 64)
                if n >= EARLY:
                    pe.wait_ge(g.w_lo, n - EARLY + 1)
                for i, src in enumerate(srcs):
                    ins = te.transpose(bank[n % EARLY][:, i * P:(i + 1) * P], src, ident[:])
                ins.then_inc(g.w_ps, 1)

            pe.wait_ge(g.consts, 5)
            for n in range(EARLY):
                transpose_group(n)
            pe.wait_ge(g.small_in, 16 * 9)
            te.transpose(bank[7][:, 0:E], rw_raw[:], ident[0:E, 0:E]).then_inc(g.rw_ps, 1)
            pe.wait_ge(g.xn1_ready, 1)
            for i in range(8):
                if i >= 2:
                    pe.wait_ge(g.t_ev, i - 1)
                if i == 4:
                    pe.wait_ge(g.rw_ev, 1)
                    pe.wait_ge(g.t_ev, 4)
                    for k in range(NT):
                        ins = te.matmul(bank[6][:, k * E:(k + 1) * E], xn1T[:, k * P:(k + 1) * P], rwT[:], start=True, stop=True)
                    ins.then_inc(g.lg_ps, 1)
                    pe.wait_ge(g.xn2_ready, 1)
                src = xn1 if i < 4 else x_all
                for j in range(4):
                    ins = te.transpose(bank[4 + i % 2][:, j * P:(j + 1) * P], src[:, 4 * (i % 4) + j, :], ident[:])
                ins.then_inc(g.t_ps, 1)
            pe.wait_ge(g.ohs_ready, 1)
            oo = ohs[:].rearrange("p t e -> p (t e)")
            te.matmul(bank[6][:, 0:P], tri[:], oo, start=True, stop=True)
            te.matmul(bank[6][:, P:2 * P], ones[:], oo, start=True, stop=True).then_inc(g.rank_ps, 1)
            pe.wait_ge(g.n2_ready, 4)
            te.transpose(bank[7][:, 64:96], nk2[:].rearrange("p a d -> p (a d)"), ident[0:32, 0:32]).then_inc(g.n_ps, 1)
            te.transpose(bank[7][:, 96:128], nv2[:].rearrange("p a d -> p (a d)"), ident[0:32, 0:32]).then_inc(g.n_ps, 1)
            pe.wait_ge(g.nvT_ready, 3)
            pe.wait_ge(g.o_in, 16)
            for p in range(PAIRS):
                ins = te.matmul(bank[7][0:32, 256:256 + DIM], nvT[:, 32 * p:32 * p + 32], raw_o[:, p, :],
                                start=p == 0, stop=p == PAIRS - 1)
            ins.then_inc(g.u_ps, 1)
            for n in range(EARLY, len(groups)):
                transpose_group(n)

            pe.wait_ge(g.w_lo, len(groups))
            pe.wait_ge(g.wraw_lo, 3)
            pe.wait_ge(g.un_ready, 1)

            def side_job(job, b):
                kind, c, w, t, i, n = job
                nb = b + 1
                tt = slice(t * P, (t + 1) * P)
                if not isinstance(n, int) or n > 0:
                    pe.wait_ge(left[i], n)
                if kind == "kq":
                    pe.wait_ge(g.xlo, 2 * nb + 2 - w)
                    ins = three(side[i][:], [x[:, tt] for x in (xs2 if w else xs1)],
                                [x[:, c * 512:(c + 1) * 512] for x in (wq if w else wkv)], True, True)
                if kind == "tr":
                    src = (qtok if w else ktok)[t]
                    pe.wait_ge(g.kqn, 8 * (b if c else nb) + nth(c, w, t) + 1)
                    for q in range(4):
                        p = 4 * c + q
                        ins = te.transpose(side[i][:, q * P:(q + 1) * P], src[:, p * P:(p + 1) * P], ident[:])
                if kind == "v":
                    if c:
                        pe.wait_ge(g.late_lo, b + 1)
                    else:
                        pe.wait_ge(g.xlo, 2 * nb + 2)
                    ins = three(side[i][:], [x[:, tt] for x in (xs_late if c else xs1)],
                                [x[:, INNER + c * 512:INNER + (c + 1) * 512] for x in wkv], True, True)
                if kind == "sh":
                    pe.wait_ge(g.late_lo, b + 1)
                    for gu in range(2):
                        ins = three(side[i][:, gu * SEQ:(gu + 1) * SEQ],
                                    [x[:, (2 * gu + c) * P:(2 * gu + c + 1) * P] for x in sgu], [x[:] for x in xs_late], True, True)
                if kind == "pn":
                    pe.wait_ge(g.pnc, 2 * PAIRS * b)
                    for k in range(TB):
                        ins = te.transpose(side[i][0:32, k * P:(k + 1) * P], pnull[:, k, :], ident[:])
                if kind == "yt":
                    pe.wait_ge(g.yev, b)
                    for k in range(TB):
                        ins = te.transpose(side[i][:, k * P:(k + 1) * P], yT[:, k * P:(k + 1) * P], ident[:])
                ins.then_inc(filled[i], 1)

            def entry(part, b, steps=range(HEADS)):
                whose = PARTS[part]
                for s in steps:
                    todo = jobs(part, b, s)
                    h = head_at(part, s, 4)
                    if h is not None and h % 2:
                        p = h // 2
                        if part != "first" or p >= 1:
                            pe.wait_ge(g.olo, PAIRS * b + p)
                        for half, evacuated in ((0, g.ptev_d), (1, g.ptev_a)):
                            pe.wait_ge(evacuated, PAIRS * b + p + 1)
                            r, hh = slice(half * DH, (half + 1) * DH), 2 * (p % PAIRS) + half
                            te.matmul(opair[r, 0:SEQ], v[:, 0, hh * DH:(hh + 1) * DH], probT[half][:, 0:SEQ], start=True, stop=False)
                            ins = te.matmul(opair[r, P:SEQ], v[:, 1, hh * DH:(hh + 1) * DH], probT[half][:, SEQ:3 * P],
                                            start=False, stop=True)
                        ins.then_inc(g.pvd, 1)
                    h = head_at(part, s, 3)
                    if h is not None:
                        pe.wait_ge(g.pn, TB * (HEADS * b + h + 1))
                        if part != "first" or h >= 2:
                            pe.wait_ge(g.ptev_a if h % 2 else g.ptev_d, PAIRS * b + h // 2)
                        for k, c in enumerate((NNULL, K0 + NNULL, K0 + NNULL + P)):
                            ins = te.transpose(bank[2 + h % 2][:, k * P:(k + 1) * P], prob[:, h % 4, c:c + P], ident[:])
                        ins.then_inc(g.ptps, 1)
                    h = head_at(part, s, 0)
                    if h is not None:
                        if part != "first" or h >= 2:
                            pe.wait_ge(g.ttr, TB * (HEADS * b + h - 1))
                        te.matmul(bank[h % 2][:, 0:K0], qT[:, h // 2, 0:P], kT[:, h, 0:K0], start=True, stop=True)
                        te.matmul(bank[h % 2][:, K0:KS], qT[:, h // 2, P:SEQ], kT[:, h, :], start=True, stop=True).then_inc(g.sps, 1)
                    for job in todo:
                        side_job(job, b)
                    if s == 5 and "prev" in whose:
                        pe.wait_ge(g.pn_lo, b)
                        te.matmul(bank[6][:, 0:SEQ], unull[:], pnT[:], start=False, stop=False)
                    h = head_at(part, s, 6)
                    if h is not None and h % 2:
                        p = h // 2
                        if p == 0 and part != "first":
                            pe.wait_ge(g.yev, b)
                        pe.wait_ge(g.olo, PAIRS * b + p + 1)
                        three(bank[6][:, 0:SEQ], [x[:, p % PAIRS, :] for x in wo], oT[p % 2], p == 0,
                              p == -1).then_inc(g.oread, 1)
                    if s == 13 and "own" in whose:
                        pe.wait_ge(g.sh_lo, 2 * b + 2)
                        for c in range(2):
                            ins = three(bank[6][:, 0:SEQ], [x[:, c, :] for x in sd], [x[:, c * SEQ:(c + 1) * SEQ] for x in hss],
                                        False, False)
                        ins.then_inc(g.shd, 1)

            entry("ahead", -1, range(AHEAD))

            for i in range(2):
                if count("ahead", i):
                    pe.wait_ge(left[i], count("ahead", i))
            pe.wait_ge(g.slots_ready, 2)

            def expert_of(n):
                return pe.value_load(tile_expert[0:1, bass.ds(n, 1)], min_val=0, max_val=E - 1)

            def turn(it, first, drain, steps=range(MU)):
                xs, ht, gu, down = (staged(first, drain, steps, lag) for lag in (0, 4, 2, 5))
                e_of = {}
                for st in steps:
                    for use in (gu, down):
                        if st in use and use[st] not in e_of:
                            e_of[use[st]] = expert_of(it * MU + use[st])
                    if st in xs:
                        j = xs[st]
                        n = it * MU + j
                        pe.wait_ge(m_in[j % RX], 16 * (it * (MU // RX) + j // RX + 1))
                        if not first or j >= 2:
                            pe.wait_ge(g.m_xlo, n - 1)
                        te.transpose(bank[j % 2][:, 0:P], mx_in[j % RX][:], ident[:]).then_inc(g.m_xps, 1)
                    if st in ht:
                        j = ht[st]
                        n = it * MU + j
                        pe.wait_ge(g.m_h, n + 1)
                        if not first or j >= 2:
                            pe.wait_ge(g.m_hlo, n - 1)
                        for c in range(2):
                            ins = te.transpose(bank[4 + j % 2][:, c * P:(c + 1) * P], mh[j % RH][:, c * P:(c + 1) * P], ident[:])
                        ins.then_inc(g.m_hps, 1)
                    if st in gu:
                        j = gu[st]
                        n = it * MU + j
                        e = e_of[j]
                        pe.wait_ge(g.m_xlo, n + 1)
                        if not first or j >= 2:
                            pe.wait_ge(g.m_h, n - 1)
                        w = [t[:, bass.ds(e, 1), :].rearrange("p o n -> p (o n)") for t in egu]
                        three(bank[2 + j % 2][:], mxT[j % RH], w, True, True).then_inc(g.m_gups, 1)
                    if st in down:
                        j = down[st]
                        n = it * MU + j
                        e = e_of[j]
                        pe.wait_ge(g.m_hlo, n + 1)
                        if not first or j >= 2:
                            pe.wait_ge(g.m_yev, n - 1)
                        w = [t[:, bass.ds(e, 1), :].rearrange("p o n -> p (o n)") for t in ed]
                        for c in range(2):
                            cc = slice(c * P, (c + 1) * P)
                            ins = three(bank[6 + j % 2][:, 0:DIM], [x[:, cc] for x in mhT[j % 2]], [x[:, cc] for x in w],
                                        c == 0, c == 1)
                        ins.then_inc(g.m_yps, 1)

            turn(0, True, False)
            with pe.Fori(1, TURNS) as it:
                turn(it, False, False)
            turn(TURNS, False, True, range(5))

            pe.wait_ge(g.kt_null, 2)
            pe.wait_ge(g.m_yev, SLOT_TILES)
            entry("ready", -1, range(3))
            for i in range(2):
                pe.wait_ge(left[i], count("ahead", i) + count("ready", i))
            entry("first", 0)
            with pe.Fori(1, BATCH - 1) as b:
                entry("mid", b)
            entry("last", BATCH - 1)
            entry("drain", BATCH, range(DRAIN))

_INS = ['L0_attn_x', 'L0_attn_norm_g', 'L0_attn_norm_b', 'L0_attn_Wq', 'L0_attn_Wkv', 'L0_attn_q_scale',
        'L0_attn_k_scale', 'L0_attn_null_kv', 'L0_attn_Wout', 'L0_ffn_sg_w', 'L0_ffn_su_w', 'L0_ffn_sd_w',
        'L0_ffn_router_w', 'L0_ffn_routing_bias', 'L0_ffn_wg', 'L0_ffn_wu', 'L0_ffn_wd']


def kernel(**inputs):
    import numpy as _np
    import concourse.bacc as _bacc
    from concourse import mybir as _mybir
    from concourse.bass_utils import run_bass_kernel_spmd as _run

    nc = _bacc.Bacc("TRN2", target_bir_lowering=False, num_devices=1)
    arrays, args = {}, {}
    for name in _INS:
        a = _np.ascontiguousarray(inputs[name])
        arrays[f"in_{name}_dram"] = a
        args[name] = nc.dram_tensor(f"in_{name}_dram", a.shape, _mybir.dt.from_np(a.dtype), kind="ExternalInput").ap()
    out = nc.dram_tensor("out_0_dram", inputs['L0_attn_x'].shape, _mybir.dt.float32, kind="ExternalOutput").ap()
    build(nc, args, out)
    r = _run(nc, [arrays], core_ids=[0])
    return r.results[0]["out_0_dram"]
```
